# Optimizing a Trainium2 kernel written in Bass

```python
import numpy as np
import jax
import jax.numpy as jnp

def _softmax(x, axis=-1):
    return jax.nn.softmax(x, axis=axis)

def _gelu(x):
    return jax.nn.gelu(x, approximate=True)

def _silu(x):
    return jax.nn.silu(x)

def _sigmoid(x):
    return jax.nn.sigmoid(x)

def _layernorm(x, axis=-1, eps=1e-05):
    m = jnp.mean(x, axis=axis, keepdims=True)
    v = jnp.var(x, axis=axis, keepdims=True)
    return (x - m) / jnp.sqrt(v + eps)

def _scatter_add(tgt, idx, src, axis=0):
    return tgt.at[idx].add(src)

def _segment_sum(src, seg, n):
    return jax.ops.segment_sum(src, seg, n)
kernel_name = 'mk_xattn_ffn_d1_seqx_r8_7d802f'

def setup_inputs(seed: int=0):
    np.random.seed(seed)
    _w = jnp.asarray

    def _rec_inputs():
        import jax
        import jax.numpy as jnp
        _rk = jax.random.key(seed)
        x = 7.22e-05 + 1 * jax.random.normal(jax.random.fold_in(_rk, 1), (8, 56, 128), jnp.float32)
        _lenS = 56 - jax.random.randint(jax.random.fold_in(_rk, 7), (8,), 0, max(1, 56 // 4) + 1, jnp.int32)
        _lenS2 = 1500 - jax.random.randint(jax.random.fold_in(_rk, 8), (8,), 0, max(1, 1500 // 4) + 1, jnp.int32)
        _ctx_768P = jax.random.normal(jax.random.fold_in(_rk, 11), (8, 16, 96), jnp.float32)
        _ctx_768c = jax.random.dirichlet(jax.random.fold_in(_rk, 511), 0.3 * jnp.ones((16,), jnp.float32), (8, 1500))
        _ctx_768t = jnp.einsum('bsk,bkd->bsd', _ctx_768c, _ctx_768P)
        _ctx_768t = _ctx_768t * jax.lax.rsqrt(jnp.mean(jnp.square(_ctx_768t)) + 1e-12) * 0.953939
        ctx_768 = 2.09791e-05 + 1.00001 * (_ctx_768t + 0.3 * jax.random.normal(jax.random.fold_in(_rk, 611), (8, 1500, 96), jnp.float32))
        return (x, ctx_768)
    x, ctx_768 = _rec_inputs()

    def _L0_xattn_setup():
        import jax, jax.numpy as jnp
        import numpy as np
        HEADS = 8
        DIM_HEAD = 64
        SCALE = DIM_HEAD ** (-0.5)
        key = jax.random.key(seed)
        ks = jax.random.split(key, 7)
        b, n, m = (4, 256, 128)
        qd, cd, inner = (128, 96, HEADS * DIM_HEAD)
        s = lambda fan_in: 1.0 / np.sqrt(fan_in)
        return {'x': jax.random.normal(ks[0], (b, n, qd), jnp.float32), 'context': jax.random.normal(ks[1], (b, m, cd), jnp.float32), 'Wq': jax.random.normal(ks[2], (qd, inner), jnp.float32) * s(qd), 'Wk': jax.random.normal(ks[3], (cd, inner), jnp.float32) * s(cd), 'Wv': jax.random.normal(ks[4], (cd, inner), jnp.float32) * s(cd), 'Wout': jax.random.normal(ks[5], (inner, qd), jnp.float32) * s(inner), 'bout': jax.random.normal(ks[6], (qd,), jnp.float32) * 0.01}
    _L0_xattn_all = _L0_xattn_setup()
    _L0_xattn_in = {k: v for k, v in _L0_xattn_all.items() if k in ('Wq', 'Wk', 'Wv', 'Wout', 'bout')}
    del _L0_xattn_all

    def _L0_ffn_setup():
        import jax, jax.numpy as jnp
        import numpy as np
        QMAX = 127.0

        def _ste_round(v):
            return v + jax.lax.stop_gradient(jnp.round(v) - v)

        def _act_fake_quant(x, clip_factor):
            scale = jax.nn.sigmoid(clip_factor) * jnp.max(jnp.abs(x)) / QMAX
            return jnp.clip(_ste_round(x / scale), -QMAX - 1.0, QMAX) * scale

        def _weight_fake_quant(w):
            scale = jnp.max(jnp.abs(w), axis=1, keepdims=True) / QMAX
            return jnp.clip(_ste_round(w / scale), -QMAX - 1.0, QMAX) * scale
        key = jax.random.key(seed)
        k1, k2, k3, k4 = jax.random.split(key, 4)
        B, S, H, I = (8, 1024, 128, 352)
        return {'x': jax.random.normal(k1, (B, S, H), dtype=jnp.float32), 'clip_x': jnp.full((1,), 4.0, dtype=jnp.float32), 'clip_down': jnp.full((1,), 4.0, dtype=jnp.float32), 'w_gate': jax.random.normal(k2, (I, H), dtype=jnp.float32) * 0.02, 'w_up': jax.random.normal(k3, (I, H), dtype=jnp.float32) * 0.02, 'w_down': jax.random.normal(k4, (H, I), dtype=jnp.float32) * 0.02}
    _L0_ffn_all = _L0_ffn_setup()
    _L0_ffn_in = {k: v for k, v in _L0_ffn_all.items() if k in ('clip_x', 'clip_down', 'w_gate', 'w_up', 'w_down')}
    del _L0_ffn_all
    return {'x': x, 'ctx_768': ctx_768, 'L0_xattn_Wq': _L0_xattn_in['Wq'], 'L0_xattn_Wk': _L0_xattn_in['Wk'], 'L0_xattn_Wv': _L0_xattn_in['Wv'], 'L0_xattn_Wout': _L0_xattn_in['Wout'], 'L0_xattn_bout': _L0_xattn_in['bout'], 'L0_ffn_clip_x': _L0_ffn_in['clip_x'], 'L0_ffn_clip_down': _L0_ffn_in['clip_down'], 'L0_ffn_w_gate': _L0_ffn_in['w_gate'], 'L0_ffn_w_up': _L0_ffn_in['w_up'], 'L0_ffn_w_down': _L0_ffn_in['w_down']}

def reference(x, ctx_768, L0_xattn_Wq, L0_xattn_Wk, L0_xattn_Wv, L0_xattn_Wout, L0_xattn_bout, L0_ffn_clip_x, L0_ffn_clip_down, L0_ffn_w_gate, L0_ffn_w_up, L0_ffn_w_down):
    import jax
    import jax.numpy as jnp

    def _L0_xattn_ref(x, context, Wq, Wk, Wv, Wout, bout):
        import jax, jax.numpy as jnp
        import numpy as np
        HEADS = 8
        DIM_HEAD = 64
        SCALE = DIM_HEAD ** (-0.5)
        b, n, _ = x.shape
        m = context.shape[1]
        q = (x @ Wq).reshape(b, n, HEADS, DIM_HEAD)
        k = (context @ Wk).reshape(b, m, HEADS, DIM_HEAD)
        v = (context @ Wv).reshape(b, m, HEADS, DIM_HEAD)
        sim = jnp.einsum('bihd,bjhd->bhij', q, k) * SCALE
        attn = jax.nn.softmax(sim, axis=-1)
        out = jnp.einsum('bhij,bjhd->bihd', attn, v).reshape(b, n, HEADS * DIM_HEAD)
        return out @ Wout + bout

    def _L0_ffn_ref(x, clip_x, clip_down, w_gate, w_up, w_down):
        import jax, jax.numpy as jnp
        import numpy as np
        QMAX = 127.0

        def _ste_round(v):
            return v + jax.lax.stop_gradient(jnp.round(v) - v)

        def _act_fake_quant(x, clip_factor):
            scale = jax.nn.sigmoid(clip_factor) * jnp.max(jnp.abs(x)) / QMAX
            return jnp.clip(_ste_round(x / scale), -QMAX - 1.0, QMAX) * scale

        def _weight_fake_quant(w):
            scale = jnp.max(jnp.abs(w), axis=1, keepdims=True) / QMAX
            return jnp.clip(_ste_round(w / scale), -QMAX - 1.0, QMAX) * scale
        xq = _act_fake_quant(x, clip_x[0])
        gate = jnp.einsum('bsh,ih->bsi', xq, _weight_fake_quant(w_gate))
        up = jnp.einsum('bsh,ih->bsi', xq, _weight_fake_quant(w_up))
        h = _act_fake_quant(jax.nn.silu(gate) * up, clip_down[0])
        return jnp.einsum('bsi,hi->bsh', h, _weight_fake_quant(w_down))
    x = x + _L0_xattn_ref(_layernorm(x, axis=-1), ctx_768, L0_xattn_Wq, L0_xattn_Wk, L0_xattn_Wv, L0_xattn_Wout, L0_xattn_bout)
    x = x + _L0_ffn_ref(_layernorm(x, axis=-1), L0_ffn_clip_x, L0_ffn_clip_down, L0_ffn_w_gate, L0_ffn_w_up, L0_ffn_w_down)
    return x

_drawn_inputs = setup_inputs


def setup_inputs(seed=0):
    import zlib

    import numpy as np

    out = dict(_drawn_inputs(seed))
    spreads = {}
    factors = {'L0_xattn_bout': 5.997,
     'L0_ffn_w_gate': 5.712,
     'L0_ffn_w_up': 5.062,
     'L0_ffn_w_down': 5.111}
    for name, (base, spread) in spreads.items():
        noise = np.random.default_rng([zlib.crc32(name.encode()), seed]).standard_normal(out[name].shape)
        drawn = base * np.exp(spread * noise) if base else spread * noise
        out[name] = jnp.asarray(drawn.astype(out[name].dtype))
    for name, factor in factors.items():
        out[name] = (out[name] * factor).astype(out[name].dtype)
    return out
```

```python
import concourse.bass as bass
from concourse import mybir
from contextlib import ExitStack

F32 = mybir.dt.float32
F32R = mybir.dt.float32r
BF16 = mybir.dt.bfloat16
ACT = mybir.ActivationFunctionType
ALU = mybir.AluOpType
AX = mybir.AxisListType

B, S, D = 8, 56, 128
M, C = 1500, 96
H, DH = 8, 64
F = 352
KT = 125
T = M // KT
HQ = H * S
G = 4
GQ = HQ // G
MC = 500
NM = M // MC
PAIRS = B // 2
TOK = 2 * S
ALLTOK = B * S
LAG = 3
RING = 4
SCALE = DH ** -0.5
EPS = 1e-5
QMAX = 127.0
ROUND = 1.5 * 2.0 ** 23
FT = [(0, 128), (128, 128), (256, 96)]


def program(nc, x_d, ctxT_d, ctx_d, wqT_d, wkT_d, wvT_d, wout_d, bout_d, clipx_d, clipd_d,
            wg_d, wu_d, wd_d, out_d):
    stack = ExitStack()
    with stack:
        def sb(name, shape, dt=F32):
            return stack.enter_context(nc.sbuf_tensor(name, shape, dt))

        def ps(name, cols=512, dt=F32):
            return stack.enter_context(nc.psum_tensor(name, [128, cols], dt))

        def sem(name):
            return stack.enter_context(nc.semaphore(name))

        ident = sb("ident", [128, 128])
        ident16 = sb("ident16", [128, 128], BF16)
        wqT, wkT = sb("wqT", [DH, H, D]), sb("wkT", [DH, H, C])
        wvT, wout = sb("wvT", [DH, H, C]), sb("wout", [DH, H, D])
        wqk = sb("wqk", [D, H, C])
        wvo = sb("wvo", [C, H, D])
        bout = sb("bout", [TOK, D])
        clips = sb("clips", [128, 2])
        sig127 = sb("sig127", [128, 2])
        x_in = sb("x_in", [TOK, PAIRS, D])
        xb = sb("xb", [TOK, PAIRS, D])
        stats = sb("stats", [TOK, PAIRS, 6])
        mv = sb("mv", [TOK, PAIRS, 2])
        rstd = sb("rstd", [TOK, PAIRS])
        veps = sb("veps", [TOK, PAIRS])
        nt = sb("nt", [TOK, PAIRS])
        minus_half = sb("minus_half", [TOK, PAIRS])
        xn = sb("xn", [TOK, PAIRS, D])
        xnT = sb("xnT", [D, ALLTOK])
        x1_now = sb("x1_now", [TOK, D])
        x1 = sb("x1", [TOK, PAIRS, D])
        xh = sb("xh", [TOK, PAIRS, D])
        stats2, mv2 = sb("stats2", [TOK, 6]), sb("mv2", [TOK, 2])
        veps2, rstd2, nt2 = sb("veps2", [TOK, 1]), sb("rstd2", [TOK, 1]), sb("nt2", [TOK, 1])
        q_hi = sb("q_hi", [C, B, HQ], F32R)
        q_lo = sb("q_lo", [C, B, HQ], F32R)
        q_now = [sb(f"q_now{p}", [C + 1, HQ], F32R) for p in range(2)]
        ctxT_in = [sb(f"ctxT_in{p}", [C, M]) for p in range(2)]
        ctxT_hi = [sb(f"ctxT_hi{p}", [C + 1, M], F32R) for p in range(2)]
        ctxT_lo = [sb(f"ctxT_lo{p}", [C, M], F32R) for p in range(2)]
        ctx_in = [sb(f"ctx_in{p}", [KT, T, C]) for p in range(2)]
        ctx_hi = [sb(f"ctx_hi{p}", [KT, T, D], F32R) for p in range(2)]
        ctx_lo = [sb(f"ctx_lo{p}", [KT, T, C], F32R) for p in range(2)]
        maxima = [sb(f"maxima{p}", [GQ, G]) for p in range(2)]
        e_full = sb("e_full", [KT, RING, HQ])
        e_hi = sb("e_hi", [KT, RING, HQ], F32R)
        e_lo = sb("e_lo", [KT, RING, HQ], F32R)
        den_t = sb("den_t", [32, HQ])
        inv_t = sb("inv_t", [C, HQ // 32])
        inv = sb("inv", [C, HQ])
        attn = sb("attn", [C, H, 2, S])
        wg, wu = sb("wg", [128, 3, D]), sb("wu", [128, 3, D])
        wd = sb("wd", [D, F])
        wg_q, wu_q = sb("wg_q", [128, 3, D], BF16), sb("wu_q", [128, 3, D], BF16)
        wd_q = sb("wd_q", [D, F], BF16)
        wt = sb("wt", [128, F + 32])
        wgT, wuT = sb("wgT", [D, F], BF16), sb("wuT", [D, F], BF16)
        wdT = sb("wdT", [128, 3, D], BF16)
        wmax = sb("wmax", [128, 7])
        wscale, winv = sb("wscale", [128, 7]), sb("winv", [128, 7])
        wd_row = sb("wd_row", [TOK, D])
        xmax = sb("xmax", [TOK, PAIRS])
        xmax1 = sb("xmax1", [TOK, 1])
        xs = sb("xs", [128, 3])
        xscale = sb("xscale", [128, 6])
        xhT = sb("xhT", [D, ALLTOK])
        xt1, xt2 = sb("xt1", [D, ALLTOK]), sb("xt2", [D, ALLTOK])
        xq = sb("xq", [D, ALLTOK], BF16)
        silu = sb("silu", [128, 3, ALLTOK])
        hh = sb("hh", [128, 3, ALLTOK])
        hmax = sb("hmax", [128, 3])
        hmax1 = sb("hmax1", [128, 1])
        hs = sb("hs", [128, 3])
        ht1, ht2 = sb("ht1", [128, 3, ALLTOK]), sb("ht2", [128, 3, ALLTOK])
        hq = sb("hq", [128, 3, ALLTOK], BF16)
        y = sb("y", [TOK, PAIRS, D])
        warm = sb("warm", [1, 2])

        p_s = [ps(f"p_s{i}") for i in range(2)]
        p_m = ps("p_m", NM * 512)
        p_o = [ps(f"p_o{i}") for i in range(2)]
        p_x = ps("p_x")

        p_mb = [p_m[:, 512 * i:512 * i + 512] for i in range(NM)]
        q_banks = [p_s[0], p_s[1], p_o[0], p_o[1]]
        g_banks = [p_s[0], p_s[1], p_o[0]]
        u_banks = p_mb

        names = """x_loaded qk_loaded vo_loaded bias_loaded ffn_loaded ident_made consts_made
            ln_step pow_made xn_made xnT_made xnT_copied wqk_made wqk_copied wvo_made wvo_copied
            q_made q_hi_made q_lo_made ones_made q_copied
            ctxT_hi_made ctxT_lo_made ctx_hi_made ctx_lo_made
            max_scored max_made scored exp_made lo_made pv_done norm_step attn_made
            projected x1_made ln2_step veps2_made pow2_made xh_made
            w_step wmax_made w_quantised wT_made wT_copied row_made row_copied clip_exp clip_step
            xhT_made xhT_copied xmax_step xmax_spread x_quantised gate_made up_made silu_made h_step
            hmax_ready hmax_spread h_step2 h_quantised y_made y_step out_stored act_warm""".split()
        sems = {n: sem(n) for n in names}
        s = type("Sems", (), sems)
        ctxT_loaded = [sem(f"ctxT_loaded{p}") for p in range(2)]
        ctx_loaded = [sem(f"ctx_loaded{p}") for p in range(2)]
        max_moved = [sem(f"max_moved{p}") for p in range(2)]

        block = stack.enter_context(nc.Block())

        def batches(eng, batch):
            batch(0, 0, 0, True, False)
            with eng.Fori(1, PAIRS) as i:
                batch(2 * i - 1, 1, i - 1, False, False)
                batch(2 * i, 0, i, False, False)
            batch(B - 1, 1, PAIRS - 1, False, True)

        @block.sync
        def _(sp):
            def load_ctx(b, par, half):
                sp.dma_start(ctxT_in[par][:, :], ctxT_d[bass.ds(b, 1), :, :].rearrange("o c m -> (o c) m"))\
                    .then_inc(ctxT_loaded[par], 16)
                sp.dma_start(ctx_in[par][:, :, :].rearrange("k t c -> k (t c)"),
                             ctx_d[bass.ds(b, 1), :, :].rearrange("o k n -> (o k) n"))\
                    .then_inc(ctx_loaded[par], 16)

            def move_max(b, par):
                for g in range(G):
                    sp.wait_ge(s.max_made, G * b + g + 1)
                    sp.dma_start(q_now[par][C:C + 1, g * GQ:(g + 1) * GQ].bitcast(F32),
                                 maxima[par][:, g:g + 1]).then_inc(max_moved[par], 16)

            sp.dma_start(x_in[:, :, :], x_d).then_inc(s.x_loaded, 16)
            load_ctx(0, 0, 0)
            load_ctx(1, 1, 0)
            sp.dma_start(bout[:, :], bout_d).then_inc(s.bias_loaded, 16)
            move_max(0, 0)

            def load_second_next(b, par, half):
                sp.wait_ge(s.ctxT_lo_made, b + 1)
                sp.wait_ge(s.ctx_lo_made, b + 1)
                load_ctx(b + 2, par, half)

            load_second_next(0, 0, 0)
            move_max(1, 1)
            with sp.Fori(1, PAIRS - 1) as i:
                load_second_next(2 * i - 1, 1, i)
                move_max(2 * i, 0)
                load_second_next(2 * i, 0, i)
                move_max(2 * i + 1, 1)
            load_second_next(B - 3, 1, 0)
            move_max(B - 2, 0)
            move_max(B - 1, 1)
            sp.wait_ge(s.y_step, 2)
            sp.dma_start(out_d, y[:, :, :]).then_inc(s.out_stored, 16)
            sp.wait_ge(s.out_stored, 16)

        @block.gpsimd
        def _(pool):
            pool.memset(ident[:, :], 0.0).then_inc(s.ident_made, 1)
            pool.wait_ge(s.ident_made, 1)
            pool.memset(minus_half[:, :], -0.5).then_inc(s.consts_made, 1)
            pool.wait_ge(s.consts_made, 1)
            pool.affine_select(out=ident[:, :], in_=ident[:, :], compare_op=ALU.not_equal, fill=1.0,
                               base=0, pattern=[[-1, 128]], channel_multiplier=1).then_inc(s.ident_made, 1)
            pool.wait_ge(s.ident_made, 2)
            pool.tensor_copy(ident16[:, :], ident[:, :]).then_inc(s.ident_made, 1)
            pool.wait_ge(s.ident_made, 3)
            pool.wait_ge(s.ln_step, 3)
            pool.tensor_tensor(rstd[:, :], veps[:, :], minus_half[:, :], ALU.pow).then_inc(s.pow_made, 1)
            pool.wait_ge(s.pow_made, 1)
            for p in range(2):
                pool.memset(ctxT_hi[p][C:C + 1, :].bitcast(F32), -1.0).then_inc(s.ones_made, 1)
                pool.wait_ge(s.ones_made, 2 * p + 1)
                pool.memset(ctx_hi[p][:, :, C:D].bitcast(F32), 1.0).then_inc(s.ones_made, 1)
                pool.wait_ge(s.ones_made, 2 * p + 2)
            pool.dma_start(wg[:, 0:2, :], wg_d[0:256, :].rearrange("(t p) h -> p t h", p=128)).then_inc(s.ffn_loaded, 16)
            pool.dma_start(wg[0:96, 2, :], wg_d[256:F, :]).then_inc(s.ffn_loaded, 16)
            pool.dma_start(wu[:, 0:2, :], wu_d[0:256, :].rearrange("(t p) h -> p t h", p=128)).then_inc(s.ffn_loaded, 16)
            pool.dma_start(wu[0:96, 2, :], wu_d[256:F, :]).then_inc(s.ffn_loaded, 16)
            pool.dma_start(wd[:, :], wd_d).then_inc(s.ffn_loaded, 16)

            def batch(b, par, half, first, last):
                for t in range(T):
                    n = T * b + t
                    k = (t) % RING
                    pool.wait_ge(s.exp_made, 2 * n + 2)
                    pool.tensor_tensor(e_lo[:, k, :], e_full[:, k, :], e_hi[:, k, :], ALU.subtract)\
                        .then_inc(s.lo_made, 1)
                    if not first and not last and par == 0 and t == 9:
                        pool.wait_ge(s.veps2_made, half)
                        pool.tensor_tensor(rstd2[:, :], veps2[:, :], minus_half[:, 0:1], ALU.pow)\
                            .then_inc(s.pow2_made, 1)

            batches(pool, batch)
            pool.wait_ge(s.veps2_made, PAIRS)
            pool.tensor_tensor(rstd2[:, :], veps2[:, :], minus_half[:, 0:1], ALU.pow).then_inc(s.pow2_made, 1)

        @block.scalar
        def _(act):
            act.dma_start(wqT[:, :, :], wqT_d).then_inc(s.qk_loaded, 16)
            act.dma_start(wkT[:, :, :], wkT_d).then_inc(s.qk_loaded, 16)
            act.dma_start(wvT[:, :, :], wvT_d).then_inc(s.vo_loaded, 16)
            act.dma_start(wout[:, :, :], wout_d).then_inc(s.vo_loaded, 16)
            act.dma_start(clips[:, 0:1], clipx_d).then_inc(s.bias_loaded, 16)
            act.dma_start(clips[:, 1:2], clipd_d).then_inc(s.bias_loaded, 16)
            for k in range(2):
                act.wait_ge(s.wqk_made, k + 1)
                act.activation(wqk[:, 4 * k:4 * k + 4, :],
                               p_mb[k][:, 0:4 * C].rearrange("p (h c) -> p h c", c=C), ACT.Copy)\
                    .then_inc(s.wqk_copied, 1)
            for k, bank in ((0, p_mb[2]), (1, p_s[0])):
                act.wait_ge(s.wvo_made, k + 1)
                act.activation(wvo[:, 4 * k:4 * k + 4, :],
                               bank[0:C, 0:4 * D].rearrange("p (h c) -> p h c", c=D), ACT.Copy)\
                    .then_inc(s.wvo_copied, 1)
            act.wait_ge(s.xnT_made, 1)
            act.activation(xnT[:, :], p_x[:, 0:ALLTOK], ACT.Copy).then_inc(s.xnT_copied, 1)
            for h in range(H):
                act.wait_ge(s.q_made, h + 1)
                act.activation(q_hi[:, :, h * S:(h + 1) * S],
                               q_banks[h % 4][0:C, 0:ALLTOK].rearrange("p (b i) -> p b i", i=S), ACT.Copy)\
                    .then_inc(s.q_hi_made, 1)

            def copy_q(b, par):
                act.activation(q_now[par][0:C, :], q_hi[:, bass.ds(b, 1), :].rearrange("c o n -> c (o n)"),
                               ACT.Copy).then_inc(s.q_copied, 1)

            act.wait_ge(s.q_hi_made, H)
            copy_q(0, 0)
            act.wait_ge(s.bias_loaded, 48)
            act.activation(sig127[:, :], clips[:, :], ACT.Exp, scale=-1.0).then_inc(s.clip_exp, 1)

            def batch(b, par, half, first, last):
                if not last:
                    copy_q(b + 1, 1 - par)
                for t in range(T):
                    n = T * b + t
                    k = t % RING
                    act.wait_ge(s.scored, n + 1)
                    if not (first and t < RING):
                        act.wait_ge(s.pv_done, n - RING + 1)
                    act.activation(e_hi[:, k, :], p_s[t % 2][0:KT, 0:HQ], ACT.Exp, scale=SCALE)\
                        .then_inc(s.exp_made, 1)
                    act.activation(e_full[:, k, :], p_s[t % 2][0:KT, 0:HQ], ACT.Exp, scale=SCALE)\
                        .then_inc(s.exp_made, 1)

            batches(act, batch)
            act.wait_ge(s.clip_exp, 1)
            act.activation(warm[:, :], sig127[0:1, :], ACT.Silu).then_inc(s.act_warm, 1)
            act.wait_ge(s.xhT_made, 1)
            act.activation(xhT[:, :], p_x[:, 0:ALLTOK], ACT.Copy).then_inc(s.xhT_copied, 1)
            act.wait_ge(s.xmax_step, 5)
            for f, (f0, fn) in enumerate(FT):
                act.wait_ge(s.gate_made, f + 1)
                act.activation(silu[0:fn, f, :], g_banks[f][0:fn, 0:ALLTOK], ACT.Silu,
                               scale=xscale[0:fn, f:f + 1]).then_inc(s.silu_made, 1)

        @block.vector
        def _(dve):
            dve.wait_ge(s.x_loaded, 16)
            for p in range(PAIRS):
                last = dve.bn_stats(stats[:, p, :], x_in[:, p, :])
            last.then_inc(s.ln_step, 1)
            dve.wait_ge(s.ln_step, 1)
            for p in range(PAIRS):
                last = dve.bn_aggr(mv[:, p, :], stats[:, p, :])
            last.then_inc(s.ln_step, 1)
            dve.wait_ge(s.ln_step, 2)
            dve.tensor_scalar(veps[:, :], mv[:, :, 1], EPS, None, ALU.add).then_inc(s.ln_step, 1)
            dve.wait_ge(s.ln_step, 3)
            dve.wait_ge(s.pow_made, 1)
            newton(dve, rstd[:, :], nt[:, :], veps[:, :], s.ln_step, 3)
            for p in range(PAIRS):
                dve.tensor_scalar(xn[:, p, :], x_in[:, p, :], mv[:, p, 0:1], rstd[:, p:p + 1],
                                  ALU.subtract, ALU.mult).then_inc(s.xn_made, 1)

            def split_ctxT_hi(b, par, half, first=False):
                dve.wait_ge(ctxT_loaded[par], 16 * half + 16)
                if not first:
                    dve.wait_ge(s.scored, T * (b - 1))
                dve.tensor_copy(ctxT_hi[par][0:C, :], ctxT_in[par][:, :]).then_inc(s.ctxT_hi_made, 1)

            def split_ctxT_lo(b, par):
                dve.wait_ge(s.ctxT_hi_made, b + 1)
                dve.tensor_tensor(ctxT_lo[par][:, :], ctxT_in[par][:, :], ctxT_hi[par][0:C, :], ALU.subtract)\
                    .then_inc(s.ctxT_lo_made, 1)

            def split_ctx_hi(b, par, half, first=False):
                dve.wait_ge(ctx_loaded[par], 16 * half + 16)
                if not first:
                    dve.wait_ge(s.pv_done, T * (b - 1))
                dve.tensor_copy(ctx_hi[par][:, :, 0:C], ctx_in[par][:, :, :]).then_inc(s.ctx_hi_made, 1)

            def split_ctx_lo(b, par):
                dve.wait_ge(s.ctx_hi_made, b + 1)
                dve.tensor_tensor(ctx_lo[par][:, :, :], ctx_in[par][:, :, :], ctx_hi[par][:, :, 0:C],
                                  ALU.subtract).then_inc(s.ctx_lo_made, 1)

            def take_max(b, par, g):
                dve.wait_ge(s.max_scored, G * b + g + 1)
                dve.reduce_max(maxima[par][:, g:g + 1],
                               p_m[0:GQ, :].rearrange("p (m k) -> p m k", k=512)[:, :, 0:MC], AX.XY)\
                    .then_inc(s.max_made, 1)

            split_ctxT_hi(0, 0, 0, True)
            for h in range(H):
                dve.wait_ge(s.q_hi_made, h + 1)
                dve.tensor_tensor(q_lo[:, :, h * S:(h + 1) * S],
                                  q_banks[h % 4][0:C, 0:ALLTOK]
                                  .rearrange("p (b i) -> p b i", i=S),
                                  q_hi[:, :, h * S:(h + 1) * S], ALU.subtract).then_inc(s.q_lo_made, 1)
            split_ctxT_lo(0, 0)
            for g in range(G):
                take_max(0, 0, g)
            split_ctx_hi(0, 0, 0, True)
            split_ctx_lo(0, 0)

            def normalise(b, par):
                base = 5 * b
                dve.wait_ge(s.pv_done, T * b + T)
                dve.transpose(den_t[:, :], p_o[par][C:128, 0:HQ]).then_inc(s.norm_step, 1)
                dve.wait_ge(s.norm_step, base + 1)
                dve.reciprocal(inv_t[0:32, :], den_t[:, :].rearrange("p (k j) -> p k j", j=32)[:, :, 0])\
                    .then_inc(s.norm_step, 1)
                dve.wait_ge(s.norm_step, base + 2)
                dve.tensor_copy(inv_t[32:64, :], inv_t[0:32, :]).then_inc(s.norm_step, 1)
                dve.tensor_copy(inv_t[64:96, :], inv_t[0:32, :]).then_inc(s.norm_step, 1)
                dve.wait_ge(s.norm_step, base + 4)
                dve.transpose(inv[:, :], inv_t[:, :].unsqueeze(2).to_broadcast([C, HQ // 32, 32]))\
                    .then_inc(s.norm_step, 1)
                dve.wait_ge(s.norm_step, base + 5)
                dve.tensor_tensor(attn[:, :, par, :], p_o[par][0:C, 0:HQ].rearrange("p (h i) -> p h i", i=S),
                                  inv[:, :].rearrange("p (h i) -> p h i", i=S), ALU.mult)\
                    .then_inc(s.attn_made, 1)

            def residual(p):
                dve.wait_ge(s.projected, p + 1)
                dve.tensor_tensor(x1_now[:, :], p_x[0:TOK, 0:D],
                                  xb[:, bass.ds(p, 1), :].rearrange("t o n -> t (o n)"), ALU.add)\
                    .then_inc(s.x1_made, 1)
                dve.wait_ge(s.x1_made, p + 1)
                dve.bn_stats(stats2[:, :], x1_now[:, :]).then_inc(s.ln2_step, 1)
                dve.wait_ge(s.ln2_step, 6 * p + 1)
                dve.tensor_scalar(x1[:, bass.ds(p, 1), :].rearrange("t o n -> t (o n)"), x1_now[:, :],
                                  1.0, None, ALU.mult)
                dve.bn_aggr(mv2[:, :], stats2[:, :]).then_inc(s.ln2_step, 1)
                dve.wait_ge(s.ln2_step, 6 * p + 2)
                dve.tensor_scalar(veps2[:, :], mv2[:, 1:2], EPS, None, ALU.add).then_inc(s.veps2_made, 1)

            def layernorm2(p):
                dve.wait_ge(s.pow2_made, p + 1)
                newton(dve, rstd2[:, :], nt2[:, :], veps2[:, :], s.ln2_step, 6 * p + 2)
                dve.tensor_scalar(xh[:, bass.ds(p, 1), :].rearrange("t o n -> t (o n)"), x1_now[:, :],
                                  mv2[:, 0:1], rstd2[:, :], ALU.subtract, ALU.mult).then_inc(s.xh_made, 1)

            dve.memset(hmax[:, :], 0.0).then_inc(s.attn_made, 1)
            dve.wait_ge(s.bias_loaded, 48)
            dve.tensor_tensor(xb[:, :, :], x_in[:, :, :],
                              bout[:, :].unsqueeze(1).to_broadcast([TOK, PAIRS, D]), ALU.add)
            dve.wait_ge(s.clip_exp, 1)
            dve.tensor_scalar(sig127[:, :], sig127[:, :], 1.0, QMAX, ALU.add, ALU.mult).then_inc(s.clip_step, 1)
            dve.wait_ge(s.clip_step, 1)
            dve.reciprocal(sig127[:, :], sig127[:, :]).then_inc(s.clip_step, 1)

            def quantise_weights():
                dve.wait_ge(s.ffn_loaded, 80)
                dve.memset(wmax[:, :], 1.0).then_inc(s.w_step, 1)
                dve.wait_ge(s.w_step, 1)
                for k, w in ((0, wg), (3, wu)):
                    dve.reduce_max(wmax[:, k:k + 2], w[:, 0:2, :], AX.X, apply_absolute_value=True)
                    dve.reduce_max(wmax[0:96, k + 2:k + 3], w[0:96, 2, :], AX.X, apply_absolute_value=True)
                dve.reduce_max(wmax[:, 6:7], wd[:, :], AX.X, apply_absolute_value=True).then_inc(s.w_step, 1)
                dve.wait_ge(s.w_step, 2)
                dve.tensor_scalar(wscale[:, :], wmax[:, :], 1.0 / QMAX, None, ALU.mult).then_inc(s.w_step, 1)
                dve.wait_ge(s.w_step, 3)
                dve.reciprocal(winv[:, :], wscale[:, :]).then_inc(s.w_step, 1)
                n = 4
                dve.wait_ge(s.w_step, n)
                jobs = [(wg[0:fn, f, :], wg_q[0:fn, f, :], winv[0:fn, f:f + 1]) for f, (_, fn) in enumerate(FT)]
                jobs += [(wu[0:fn, f, :], wu_q[0:fn, f, :], winv[0:fn, 3 + f:4 + f]) for f, (_, fn) in enumerate(FT)]
                jobs += [(wd[:, :], wd_q[:, :], winv[:, 6:7])]
                for w, q, r in jobs:
                    fn, cols = w.shape[0], w.shape[1]
                    tmp = wt[0:fn, 0:cols]
                    dve.tensor_scalar(tmp, w, r, ROUND, ALU.mult, ALU.add).then_inc(s.w_step, 1)
                    dve.wait_ge(s.w_step, n + 1)
                    dve.tensor_scalar(tmp, tmp, ROUND + QMAX, ROUND - QMAX - 1, ALU.min, ALU.max)\
                        .then_inc(s.w_step, 1)
                    dve.wait_ge(s.w_step, n + 2)
                    dve.tensor_scalar(q, tmp, ROUND, None, ALU.subtract).then_inc(s.w_step, 1)
                    n += 3
                    dve.wait_ge(s.w_step, n)

            def batch(b, par, half, first, last):
                nxt, nhalf = b + 1, half + par
                if not last:
                    split_ctxT_hi(nxt, 1 - par, nhalf, first)
                    take_max(nxt, 1 - par, 0)
                if not first:
                    normalise(b - 1, 1 - par)
                else:
                    quantise_weights()
                if not last:
                    take_max(nxt, 1 - par, 1)
                    split_ctx_hi(nxt, 1 - par, nhalf, first)
                    take_max(nxt, 1 - par, 2)
                if not first and par == 0:
                    residual(half - 1)
                if not last:
                    take_max(nxt, 1 - par, 3)
                    split_ctxT_lo(nxt, 1 - par)
                    split_ctx_lo(nxt, 1 - par)
                if not first and par == 0:
                    layernorm2(half - 1)
                if first:
                    for k, dst in enumerate((wgT[:, :], wuT[:, :], wdT[:, :, :])):
                        dve.wait_ge(s.wT_made, k + 1)
                        src = p_x[:, :].bitcast(BF16)
                        if k < 2:
                            dve.tensor_copy(dst, src[:, 0:F]).then_inc(s.wT_copied, 1)
                        else:
                            dve.tensor_copy(dst[:, 0:2, :], src[:, 0:2 * D].rearrange("p (f n) -> p f n", n=D))
                            dve.tensor_copy(dst[0:96, 2, :], src[0:96, 2 * D:3 * D]).then_inc(s.wT_copied, 1)
                    dve.wait_ge(s.row_made, 1)
                    dve.tensor_copy(wd_row[:, :], p_x[0:TOK, 0:D]).then_inc(s.row_copied, 1)

            batches(dve, batch)
            dve.reduce_max(xmax[:, 0:3], xh[:, 0:3, :], AX.X, apply_absolute_value=True)
            normalise(B - 1, 1)
            residual(PAIRS - 1)
            layernorm2(PAIRS - 1)
            dve.wait_ge(s.xh_made, PAIRS)
            dve.reduce_max(xmax[:, 3:4], xh[:, 3, :], AX.X, apply_absolute_value=True).then_inc(s.xmax_step, 1)
            dve.wait_ge(s.xmax_step, 1)
            dve.reduce_max(xmax1[:, :], xmax[:, :], AX.X).then_inc(s.xmax_step, 1)
            dve.wait_ge(s.xmax_spread, 1)
            dve.reduce_max(xs[:, 0:1], p_mb[0][:, 0:TOK], AX.X).then_inc(s.xmax_step, 1)
            dve.wait_ge(s.xmax_step, 3)
            dve.tensor_scalar(xs[:, 1:2], xs[:, 0:1], sig127[:, 0:1], None, ALU.mult).then_inc(s.xmax_step, 1)
            dve.wait_ge(s.xmax_step, 4)
            dve.reciprocal(xs[:, 2:3], xs[:, 1:2])
            dve.tensor_scalar(xscale[:, :], wscale[:, 0:6], xs[:, 1:2], None, ALU.mult).then_inc(s.xmax_step, 1)
            dve.wait_ge(s.xmax_step, 5)
            dve.wait_ge(s.xhT_copied, 1)
            dve.tensor_scalar(xt1[:, :], xhT[:, :], xs[:, 2:3], ROUND, ALU.mult, ALU.add).then_inc(s.xmax_step, 1)
            dve.wait_ge(s.xmax_step, 6)
            dve.tensor_scalar(xt2[:, :], xt1[:, :], ROUND + QMAX, ROUND - QMAX - 1, ALU.min, ALU.max)\
                .then_inc(s.xmax_step, 1)
            dve.wait_ge(s.xmax_step, 7)
            dve.tensor_scalar(xq[:, :], xt2[:, :], ROUND, None, ALU.subtract).then_inc(s.x_quantised, 1)
            for f, (_, fn) in enumerate(FT):
                dve.wait_ge(s.up_made, f + 1)
                dve.wait_ge(s.silu_made, f + 1)
                dve.scalar_tensor_tensor(hh[0:fn, f, :], u_banks[f][0:fn, 0:ALLTOK], xscale[0:fn, 3 + f:4 + f],
                                         silu[0:fn, f, :], ALU.mult, ALU.mult).then_inc(s.h_step, 1)
                dve.wait_ge(s.h_step, f + 1)
                last = dve.reduce_max(hmax[0:fn, f:f + 1], hh[0:fn, f, :], AX.X, apply_absolute_value=True)
            last.then_inc(s.h_step, 1)
            dve.wait_ge(s.h_step, 4)
            dve.reduce_max(hmax1[:, :], hmax[:, :], AX.X).then_inc(s.hmax_ready, 1)
            dve.wait_ge(s.hmax_spread, 1)
            dve.reduce_max(hs[:, 0:1], p_x[:, 0:128], AX.X).then_inc(s.h_step, 1)
            dve.wait_ge(s.h_step, 5)
            dve.tensor_scalar(hs[:, 1:2], hs[:, 0:1], sig127[:, 1:2], None, ALU.mult).then_inc(s.h_step, 1)
            dve.wait_ge(s.h_step, 6)
            dve.reciprocal(hs[:, 2:3], hs[:, 1:2]).then_inc(s.h_step, 1)
            dve.wait_ge(s.h_step, 7)
            n = 7
            for f, (_, fn) in enumerate(FT):
                dve.tensor_scalar(ht1[0:fn, f, :], hh[0:fn, f, :], hs[0:fn, 2:3], ROUND, ALU.mult, ALU.add)\
                    .then_inc(s.h_step, 1)
                dve.wait_ge(s.h_step, n + 1)
                dve.tensor_scalar(ht2[0:fn, f, :], ht1[0:fn, f, :], ROUND + QMAX, ROUND - QMAX - 1,
                                  ALU.min, ALU.max).then_inc(s.h_step, 1)
                dve.wait_ge(s.h_step, n + 2)
                dve.tensor_scalar(hq[0:fn, f, :], ht2[0:fn, f, :], ROUND, None, ALU.subtract)\
                    .then_inc(s.h_quantised, 1)
                n += 2
            dve.wait_ge(s.y_made, 1)
            dve.scalar_tensor_tensor(y[:, :, :], p_o[1][0:TOK, :].rearrange("t (p n) -> t p n", n=D), hs[0:TOK, 1:2],
                                     wd_row[:, :].unsqueeze(1).to_broadcast([TOK, PAIRS, D]), ALU.mult, ALU.mult)\
                .then_inc(s.y_step, 1)
            dve.wait_ge(s.y_step, 1)
            dve.tensor_tensor(y[:, :, :], y[:, :, :], x1[:, :, :], ALU.add).then_inc(s.y_step, 1)

        @block.tensor
        def _(pe):
            pe.wait_ge(s.qk_loaded, 32)
            for h in range(H):
                last = pe.matmul(p_mb[h // 4][:, (h % 4) * C:(h % 4 + 1) * C], wqT[:, h, :], wkT[:, h, :],
                                 start=True, stop=True)
                if h % 4 == 3:
                    last.then_inc(s.wqk_made, 1)
            pe.wait_ge(s.vo_loaded, 32)
            for h in range(H):
                bank = (p_mb[2], p_s[0])[h // 4]
                last = pe.matmul(bank[0:C, (h % 4) * D:(h % 4 + 1) * D], wvT[:, h, :], wout[:, h, :],
                                 start=True, stop=True)
                if h % 4 == 3:
                    last.then_inc(s.wvo_made, 1)
            pe.wait_ge(s.ident_made, 2)
            for p in range(PAIRS):
                pe.wait_ge(s.xn_made, p + 1)
                last = pe.transpose(p_x[:, p * TOK:(p + 1) * TOK], xn[:, p, :], ident[0:TOK, 0:TOK])
            last.then_inc(s.xnT_made, 1)
            pe.wait_ge(s.xnT_copied, 1)
            pe.wait_ge(s.wqk_copied, 2)
            pe.wait_ge(s.wvo_copied, 2)
            for h in range(H):
                if h >= 4:
                    pe.wait_ge(s.q_lo_made, h - 3)
                pe.matmul(q_banks[h % 4][0:C, 0:ALLTOK], wqk[:, h, :], xnT[:, :], start=True, stop=True)\
                    .then_inc(s.q_made, 1)

            def max_group(b, par, g, first=False):
                if g == 0:
                    pe.wait_ge(s.q_copied, b + 1)
                    pe.wait_ge(s.ctxT_hi_made, b + 1)
                if not (first and g == 0):
                    pe.wait_ge(s.max_made, G * b + g)
                for k in range(NM):
                    last = pe.matmul(p_mb[k][0:GQ, 0:MC], q_now[par][0:C, g * GQ:(g + 1) * GQ],
                                     ctxT_hi[par][0:C, k * MC:(k + 1) * MC], start=True, stop=True)
                last.then_inc(s.max_scored, 1)

            def scores(b, par, half, t, first):
                n = T * b + t
                if t == 0:
                    pe.wait_ge(max_moved[par], 16 * G * (half + 1))
                    pe.wait_ge(s.ctxT_lo_made, b + 1)
                if not (first and t < 2):
                    pe.wait_ge(s.exp_made, 2 * (n - 1))
                keys = slice(t * KT, (t + 1) * KT)
                o = p_s[t % 2][0:KT, 0:HQ]
                pe.matmul(o, ctxT_hi[par][:, keys], q_now[par][:, :], start=True, stop=False)
                pe.matmul(o, ctxT_lo[par][:, keys], q_now[par][0:C, :], start=False, stop=False)
                pe.matmul(o, ctxT_hi[par][0:C, keys], q_lo[:, bass.ds(b, 1), :].rearrange("c o n -> c (o n)"),
                          start=False, stop=True).then_inc(s.scored, 1)

            def weighted(b, par, t, early=False):
                n = T * b + t
                k = t % RING
                if t == 0:
                    pe.wait_ge(s.ctx_lo_made, b + 1)
                    if not early:
                        pe.wait_ge(s.attn_made, b)
                pe.wait_ge(s.exp_made, 2 * n + 1)
                pe.matmul(p_o[par][:, 0:HQ], ctx_hi[par][:, t, :], e_hi[:, k, :], start=(t == 0), stop=False,
                          skip_group_check=True)
                pe.matmul(p_o[par][0:C, 0:HQ], ctx_lo[par][:, t, :], e_hi[:, k, :], start=False, stop=False,
                          skip_group_check=True)
                pe.wait_ge(s.lo_made, n + 1)
                pe.matmul(p_o[par][:, 0:HQ], ctx_hi[par][:, t, :], e_lo[:, k, :], start=False, stop=(t == T - 1),
                          skip_group_check=True).then_inc(s.pv_done, 1)

            def project(p, static=False):
                pe.wait_ge(s.attn_made, 2 * p + 3)
                for h in range(H):
                    last = pe.matmul(p_x[0:TOK, 0:D], attn[:, h, :, :].rearrange("c b i -> c (b i)"), wvo[:, h, :],
                                     start=(h == 0), stop=(h == H - 1))
                last.then_inc(s.projected, 1)

            def transpose_weights(k):
                if k == 0:
                    pe.wait_ge(s.w_step, 25)
                else:
                    pe.wait_ge(s.wT_copied, k)
                o = p_x[:, :].bitcast(BF16)
                for f, (f0, fn) in enumerate(FT):
                    if k < 2:
                        last = pe.transpose(o[:, f0:f0 + fn], (wg_q, wu_q)[k][0:fn, f, :], ident16[0:fn, 0:fn])
                    else:
                        last = pe.transpose(o[0:fn, f * D:(f + 1) * D], wd_q[:, f0:f0 + fn], ident16[:, :])
                last.then_inc(s.wT_made, 1)

            for g in range(G):
                max_group(0, 0, g, first=True)
            pe.wait_ge(s.q_lo_made, H)
            pe.wait_ge(s.ones_made, 4)

            def batch(b, par, half, first, last):
                for t in range(T):
                    scores(b, par, half, t, first)
                    if not last and t in (1, 4, 6, 8):
                        max_group(b + 1, 1 - par, (1, 4, 6, 8).index(t))
                    if not first and par == 0 and t == 7:
                        project(half - 1)
                    if first and t in (9, 10, 11):
                        transpose_weights(t - 9)
                    if t >= LAG:
                        weighted(b, par, t - LAG, early=first)
                    elif not first:
                        weighted(b - 1, 1 - par, T - LAG + t)
                if first:
                    pe.wait_ge(s.wT_copied, 3)
                    pe.matmul(p_x[0:TOK, 0:D], wscale[:, 6:7].to_broadcast([D, TOK]), ident[:, :],
                              start=True, stop=True).then_inc(s.row_made, 1)

            batch(0, 0, 0, True, False)
            with pe.Fori(1, PAIRS) as i:
                batch(2 * i - 1, 1, i - 1, False, False)
                batch(2 * i, 0, i, False, False)
            batch(B - 1, 1, PAIRS - 1, False, True)
            for t in range(T - LAG, T):
                weighted(B - 1, 1, t)
            project(PAIRS - 1)
            pe.wait_ge(s.x1_made, PAIRS)
            for p in range(PAIRS):
                pe.wait_ge(s.xh_made, p + 1)
                last = pe.transpose(p_x[:, p * TOK:(p + 1) * TOK], xh[:, p, :], ident[0:TOK, 0:TOK])
            last.then_inc(s.xhT_made, 1)
            pe.wait_ge(s.xmax_step, 2)
            pe.matmul(p_mb[0][:, 0:TOK], xmax1[:, 0:1].to_broadcast([TOK, 128]), ident[0:TOK, 0:TOK],
                      start=True, stop=True).then_inc(s.xmax_spread, 1)
            pe.wait_ge(s.x_quantised, 1)
            for f, (f0, fn) in enumerate(FT):
                pe.matmul(g_banks[f][0:fn, 0:ALLTOK], wgT[:, f0:f0 + fn], xq[:, :], start=True, stop=True)\
                    .then_inc(s.gate_made, 1)
                pe.matmul(u_banks[f][0:fn, 0:ALLTOK], wuT[:, f0:f0 + fn], xq[:, :], start=True, stop=True)\
                    .then_inc(s.up_made, 1)
            pe.wait_ge(s.hmax_ready, 1)
            pe.matmul(p_x[:, 0:128], hmax1[:, 0:1].to_broadcast([128, 128]), ident[:, :],
                      start=True, stop=True).then_inc(s.hmax_spread, 1)
            pe.wait_ge(s.h_quantised, 3)
            for p in range(PAIRS):
                for f, (f0, fn) in enumerate(FT):
                    last = pe.matmul(p_o[1][0:TOK, p * D:(p + 1) * D], hq[0:fn, f, p * TOK:(p + 1) * TOK],
                                     wdT[0:fn, f, :], start=(f == 0), stop=(f == 2))
            last.then_inc(s.y_made, 1)


def newton(dve, r, t, v, step, n):
    dve.tensor_tensor(t, r, r, ALU.mult).then_inc(step, 1)
    dve.wait_ge(step, n + 1)
    dve.tensor_tensor(t, t, v, ALU.mult).then_inc(step, 1)
    dve.wait_ge(step, n + 2)
    dve.tensor_scalar(t, t, -0.5, 1.5, ALU.mult, ALU.add).then_inc(step, 1)
    dve.wait_ge(step, n + 3)
    dve.tensor_tensor(r, r, t, ALU.mult).then_inc(step, 1)
    dve.wait_ge(step, n + 4)


def kernel(x, ctx_768, L0_xattn_Wq, L0_xattn_Wk, L0_xattn_Wv, L0_xattn_Wout, L0_xattn_bout,
           L0_ffn_clip_x, L0_ffn_clip_down, L0_ffn_w_gate, L0_ffn_w_up, L0_ffn_w_down):
    import numpy as np
    from concourse import bacc
    from concourse.bass_utils import run_bass_kernel_spmd

    a = {k: np.asarray(v) for k, v in locals().items() if k not in ("np", "bacc", "run_bass_kernel_spmd")}
    ctx = a["ctx_768"]
    arrays = {
        "x_in_d": a["x"].reshape(PAIRS, TOK, D).transpose(1, 0, 2),
        "ctxT_d": ctx.transpose(0, 2, 1),
        "ctx_d": ctx.reshape(B, T, KT, C).transpose(0, 2, 1, 3).reshape(B, KT, T * C),
        "wqT_d": a["L0_xattn_Wq"].reshape(D, H, DH).transpose(2, 1, 0),
        "wkT_d": a["L0_xattn_Wk"].reshape(C, H, DH).transpose(2, 1, 0),
        "wvT_d": a["L0_xattn_Wv"].reshape(C, H, DH).transpose(2, 1, 0),
        "wout_d": a["L0_xattn_Wout"].reshape(H, DH, D).transpose(1, 0, 2),
        "bout_d": np.broadcast_to(a["L0_xattn_bout"][None], (TOK, D)),
        "clipx_d": np.broadcast_to(a["L0_ffn_clip_x"][None], (128, 1)),
        "clipd_d": np.broadcast_to(a["L0_ffn_clip_down"][None], (128, 1)),
        "wg_d": a["L0_ffn_w_gate"], "wu_d": a["L0_ffn_w_up"], "wd_d": a["L0_ffn_w_down"],
    }
    arrays = {k: np.ascontiguousarray(v) for k, v in arrays.items()}
    nc = bacc.Bacc("TRN2", target_bir_lowering=False, num_devices=1)
    args = [nc.dram_tensor(k, v.shape, mybir.dt.from_np(v.dtype), kind="ExternalInput").ap() for k, v in arrays.items()]
    out = nc.dram_tensor("out_d", (TOK, PAIRS, D), F32, kind="ExternalOutput").ap()
    program(nc, *args, out)
    r = run_bass_kernel_spmd(nc, [arrays], core_ids=[0])
    got = r.results[0]["out_d"]
    return got.transpose(1, 0, 2).reshape(B, S, D)
```

```python
import concourse.bass as bass
from concourse import mybir
from contextlib import ExitStack

F32 = mybir.dt.float32
F32R = mybir.dt.float32r
BF16 = mybir.dt.bfloat16
ACT = mybir.ActivationFunctionType
ALU = mybir.AluOpType
AX = mybir.AxisListType

B, S, D = 8, 56, 128
M, C = 1500, 96
H, DH = 8, 64
F = 352
KT = 125
T = M // KT
HQ = H * S
G = 4
GQ = HQ // G
MC = 500
NM = M // MC
CHUNKS = G * NM
PAIRS = B // 2
TOK = 2 * S
ALLTOK = B * S
LAG = 3
CTX_STEPS = (4, 6, 7, 9)
RING = 4
SCALE = DH ** -0.5
EPS = 1e-5
QMAX = 127.0
ROUND = 1.5 * 2.0 ** 23
FT = [(0, 128), (128, 128), (256, 96)]


def program(nc, x_d, ctxT_d, ctx_d, wqT_d, wkT_d, wvT_d, wout_d, bout_d, clipx_d, clipd_d,
            wg_d, wu_d, wd_d, out_d):
    stack = ExitStack()
    with stack:
        def sb(name, shape, dt=F32):
            return stack.enter_context(nc.sbuf_tensor(name, shape, dt))

        def ps(name, cols=512, dt=F32):
            return stack.enter_context(nc.psum_tensor(name, [128, cols], dt))

        def sem(name):
            return stack.enter_context(nc.semaphore(name))

        ident = sb("ident", [128, 128])
        ident16 = sb("ident16", [128, 128], BF16)
        wqT, wkT = sb("wqT", [DH, H, D]), sb("wkT", [DH, H, C])
        wvT, wout = sb("wvT", [DH, H, C]), sb("wout", [DH, H, D])
        wqk = sb("wqk", [D, H, C])
        wvo = sb("wvo", [C, H, D])
        bout = sb("bout", [TOK, D])
        clips = sb("clips", [128, 2])
        sig127 = sb("sig127", [128, 2])
        x_in = sb("x_in", [TOK, PAIRS, D])
        xb = sb("xb", [TOK, PAIRS, D])
        stats = sb("stats", [TOK, PAIRS, 6])
        mv = sb("mv", [TOK, PAIRS, 2])
        rstd = sb("rstd", [TOK, PAIRS])
        veps = sb("veps", [TOK, PAIRS])
        nt = sb("nt", [TOK, PAIRS])
        minus_half = sb("minus_half", [TOK, PAIRS])
        xn = sb("xn", [TOK, PAIRS, D])
        xnT = sb("xnT", [D, ALLTOK])
        x1_now = sb("x1_now", [TOK, D])
        x1 = sb("x1", [TOK, PAIRS, D])
        xh = sb("xh", [TOK, PAIRS, D])
        stats2, mv2 = sb("stats2", [TOK, 6]), sb("mv2", [TOK, 2])
        veps2, rstd2, nt2 = sb("veps2", [TOK, 1]), sb("rstd2", [TOK, 1]), sb("nt2", [TOK, 1])
        q_hi = sb("q_hi", [C, B, HQ], F32R)
        q_lo = sb("q_lo", [C, B, HQ], F32R)
        q_now = [sb(f"q_now{p}", [C + 1, HQ], F32R) for p in range(2)]
        ctxT_in = [sb(f"ctxT_in{p}", [C, M]) for p in range(2)]
        ctxT_hi = [sb(f"ctxT_hi{p}", [C + 1, M], F32R) for p in range(2)]
        ctxT_lo = [sb(f"ctxT_lo{p}", [C, M], F32R) for p in range(2)]
        ctx_in = [sb(f"ctx_in{p}", [KT, T, C]) for p in range(2)]
        ctx_hi = [sb(f"ctx_hi{p}", [KT, T, D], F32R) for p in range(2)]
        ctx_lo = [sb(f"ctx_lo{p}", [KT, T, C], F32R) for p in range(2)]
        chunk_max = sb("chunk_max", [GQ, G, NM])
        maxima = [sb(f"maxima{p}", [GQ, G]) for p in range(2)]
        e_full = sb("e_full", [KT, RING, HQ])
        e_hi = sb("e_hi", [KT, RING, HQ], F32R)
        e_lo = sb("e_lo", [KT, RING, HQ], F32R)
        den_t = sb("den_t", [32, HQ])
        inv_t = sb("inv_t", [C, HQ // 32])
        inv = sb("inv", [C, HQ])
        attn = sb("attn", [C, H, 2, S])
        wg, wu = sb("wg", [128, 3, D]), sb("wu", [128, 3, D])
        wd = sb("wd", [D, F])
        wg_q, wu_q = sb("wg_q", [128, 3, D], BF16), sb("wu_q", [128, 3, D], BF16)
        wd_q = sb("wd_q", [D, F], BF16)
        wt1 = sb("wt1", [128, 6 * D + F])
        wt2 = sb("wt2", [128, 6 * D + F], BF16)
        wgT, wuT = sb("wgT", [D, F], BF16), sb("wuT", [D, F], BF16)
        wdT = sb("wdT", [128, 3, D], BF16)
        wmax = sb("wmax", [128, 7])
        wscale, winv = sb("wscale", [128, 7]), sb("winv", [128, 7])
        xmax = sb("xmax", [TOK, PAIRS])
        xmax1 = sb("xmax1", [TOK, 1])
        xs = sb("xs", [128, 3])
        xscale = sb("xscale", [128, 6])
        xhT = sb("xhT", [D, ALLTOK])
        xt1, xt2 = sb("xt1", [D, ALLTOK]), sb("xt2", [D, ALLTOK], BF16)
        xq = sb("xq", [D, ALLTOK], BF16)
        silu = sb("silu", [128, 3, ALLTOK])
        hh = sb("hh", [128, 3, ALLTOK])
        hmax = sb("hmax", [128, 3])
        hmax1 = sb("hmax1", [128, 1])
        hs = sb("hs", [128, 3])
        ht1, ht2 = sb("ht1", [128, 3, ALLTOK]), sb("ht2", [128, 3, ALLTOK], BF16)
        hq = sb("hq", [128, 3, ALLTOK], BF16)
        x1T, y = sb("x1T", [D, ALLTOK]), sb("y", [D, ALLTOK])
        warm = sb("warm", [1, 2])
        filler = sb("filler", [128, 512], BF16)

        q_full = [buf[0:C, j, S:ALLTOK] for buf in (silu, hh, ht1) for j in range(3)]

        p_s = [ps(f"p_s{i}") for i in range(2)]
        p_m = ps("p_m", NM * 512)
        p_o = [ps(f"p_o{i}") for i in range(2)]
        p_x = ps("p_x")

        p_mb = [p_m[:, 512 * i:512 * i + 512] for i in range(NM)]
        q_banks = [p_s[0], p_s[1], p_o[0], p_o[1]]
        g_banks = [p_s[0], p_s[1], p_x]
        u_banks = p_mb

        names = """x_loaded qk_loaded vo_loaded bias_loaded ffn_loaded ident_made consts_made
            ln_step pow_made xn_made xnT_made xnT_copied wqk_made wqk_copied wvo_made wvo_copied
            q_made q_hi_made q_lo_made ones_made q_copied
            ctxT_hi_made ctxT_lo_made ctx_hi_made ctx_lo_made
            max_scored chunk_max_made max_made scored exp_made lo_made pv_done norm_step attn_made
            projected x1_made ln2_step veps2_made pow2_made xh_made
            w_step w_step2 warm_made first_q_made first_q_lo_made filler_made row_made w_quantised wT_made wT_copied clip_exp clip_step
            xhT_made xhT_copied xmax_step xmax3_step xscale_made xmax_spread x_quantised gate_made up_made silu_made h_step
            hmax_ready hmax_spread h_step2 q_full_made last_attn_made x1T_made x1T_copied h_quantised y_made y_step out_stored act_warm""".split()
        sems = {n: sem(n) for n in names}
        s = type("Sems", (), sems)
        ctxT_loaded = [sem(f"ctxT_loaded{p}") for p in range(2)]
        ctx_loaded = [sem(f"ctx_loaded{p}") for p in range(2)]
        max_moved = [sem(f"max_moved{p}") for p in range(2)]

        block = stack.enter_context(nc.Block())

        def batches(eng, batch):
            batch(0, 0, 0, True, False)
            with eng.Fori(1, PAIRS) as i:
                batch(2 * i - 1, 1, i - 1, False, False)
                batch(2 * i, 0, i, False, False)
            batch(B - 1, 1, PAIRS - 1, False, True)

        @block.sync
        def _(sp):
            def load_ctx(b, par, half):
                sp.dma_start(ctxT_in[par][:, :], ctxT_d[bass.ds(b, 1), :, :].rearrange("o c m -> (o c) m"))\
                    .then_inc(ctxT_loaded[par], 16)
                sp.dma_start(ctx_in[par][:, :, :].rearrange("k t c -> k (t c)"),
                             ctx_d[bass.ds(b, 1), :, :].rearrange("o k n -> (o k) n"))\
                    .then_inc(ctx_loaded[par], 16)

            def move_max(b, par):
                for g in range(G):
                    sp.wait_ge(s.max_made, G * b + g + 1)
                    sp.dma_start(q_now[par][C:C + 1, g * GQ:(g + 1) * GQ].bitcast(F32),
                                 maxima[par][:, g:g + 1]).then_inc(max_moved[par], 16)

            sp.dma_start(x_in[:, :, :], x_d).then_inc(s.x_loaded, 16)
            sp.dma_start(wqT[:, :, :], wqT_d).then_inc(s.qk_loaded, 16)
            load_ctx(0, 0, 0)
            sp.wait_ge(s.qk_loaded, 32)
            load_ctx(1, 1, 0)
            sp.dma_start(wg[:, 0:2, :], wg_d[0:256, :].rearrange("(t p) h -> p t h", p=128)).then_inc(s.ffn_loaded, 16)
            sp.dma_start(wg[0:96, 2, :], wg_d[256:F, :]).then_inc(s.ffn_loaded, 16)
            sp.dma_start(wu[:, 0:2, :], wu_d[0:256, :].rearrange("(t p) h -> p t h", p=128)).then_inc(s.ffn_loaded, 16)
            sp.dma_start(wu[0:96, 2, :], wu_d[256:F, :]).then_inc(s.ffn_loaded, 16)
            sp.dma_start(wd[:, :], wd_d).then_inc(s.ffn_loaded, 16)

            def load_second_next(b, par, half):
                sp.wait_ge(s.ctxT_lo_made, b + 1)
                sp.wait_ge(s.ctx_lo_made, b + 1)
                load_ctx(b + 2, par, half)

            load_second_next(0, 0, 0)
            move_max(1, 1)
            with sp.Fori(1, PAIRS - 1) as i:
                load_second_next(2 * i - 1, 1, i)
                move_max(2 * i, 0)
                load_second_next(2 * i, 0, i)
                move_max(2 * i + 1, 1)
            load_second_next(B - 3, 1, 0)
            move_max(B - 2, 0)
            move_max(B - 1, 1)
            sp.wait_ge(s.y_step, 2)
            sp.dma_start(out_d, y[:, :]).then_inc(s.out_stored, 16)
            sp.wait_ge(s.out_stored, 16)

        @block.gpsimd
        def _(pool):
            pool.memset(ident[:, :], 0.0).then_inc(s.ident_made, 1)
            pool.wait_ge(s.ident_made, 1)
            pool.memset(minus_half[:, :], -0.5).then_inc(s.consts_made, 1)
            pool.wait_ge(s.consts_made, 1)
            pool.affine_select(out=ident[:, :], in_=ident[:, :], compare_op=ALU.not_equal, fill=1.0,
                               base=0, pattern=[[-1, 128]], channel_multiplier=1).then_inc(s.ident_made, 1)
            pool.wait_ge(s.ident_made, 2)
            pool.tensor_copy(ident16[:, :], ident[:, :]).then_inc(s.ident_made, 1)
            pool.wait_ge(s.ident_made, 3)

            def ones(p):
                pool.memset(ctxT_hi[p][C:C + 1, :].bitcast(F32), -1.0).then_inc(s.ones_made, 1)
                pool.wait_ge(s.ones_made, 2 * p + 1)
                pool.memset(ctx_hi[p][:, :, C:D].bitcast(F32), 1.0).then_inc(s.ones_made, 1)
                pool.wait_ge(s.ones_made, 2 * p + 2)

            ones(0)
            pool.wait_ge(s.ln_step, 3)
            pool.tensor_tensor(rstd[:, :], veps[:, :], minus_half[:, :], ALU.pow).then_inc(s.pow_made, 1)
            pool.wait_ge(s.pow_made, 1)
            ones(1)
            pool.wait_ge(s.ctxT_hi_made, 1)
            pool.tensor_tensor(ctxT_lo[0][:, :], ctxT_in[0][:, :], ctxT_hi[0][0:C, :], ALU.subtract)\
                .then_inc(s.ctxT_lo_made, 1)
            for h in range(H):
                pool.wait_ge(s.q_full_made, h + 1)
                pool.tensor_tensor(q_lo[:, 1:B, h * S:(h + 1) * S],
                                   q_full[h].rearrange("p (b i) -> p b i", i=S),
                                   q_hi[:, 1:B, h * S:(h + 1) * S], ALU.subtract).then_inc(s.q_lo_made, 1)

            def batch(b, par, half, first, last):
                for t in range(T):
                    n = T * b + t
                    k = t % RING
                    pool.wait_ge(s.exp_made, 2 * n + 2)
                    pool.tensor_tensor(e_lo[:, k, :], e_full[:, k, :], e_hi[:, k, :], ALU.subtract)\
                        .then_inc(s.lo_made, 1)
                    if not first and not last and par == 0 and t == 8:
                        pool.wait_ge(s.veps2_made, half)
                        pool.tensor_tensor(rstd2[:, :], veps2[:, :], minus_half[:, 0:1], ALU.pow)\
                            .then_inc(s.pow2_made, 1)

            batches(pool, batch)
            pool.wait_ge(s.veps2_made, PAIRS)
            pool.tensor_tensor(rstd2[:, :], veps2[:, :], minus_half[:, 0:1], ALU.pow).then_inc(s.pow2_made, 1)

        @block.scalar
        def _(act):
            act.wait_ge(s.warm_made, 1)
            act.activation(warm[:, :], warm[:, :], ACT.Exp).then_inc(s.act_warm, 1)
            act.dma_start(wkT[:, :, :], wkT_d).then_inc(s.qk_loaded, 16)
            act.dma_start(clips[:, 0:1], clipx_d).then_inc(s.bias_loaded, 16)
            act.dma_start(clips[:, 1:2], clipd_d).then_inc(s.bias_loaded, 16)
            act.dma_start(bout[:, :], bout_d).then_inc(s.bias_loaded, 16)
            act.dma_start(wvT[:, :, :], wvT_d).then_inc(s.vo_loaded, 16)
            act.dma_start(wout[:, :, :], wout_d).then_inc(s.vo_loaded, 16)
            act.wait_ge(s.bias_loaded, 48)
            act.activation(sig127[:, :], clips[:, :], ACT.Exp, scale=-1.0).then_inc(s.clip_exp, 1)
            for k in range(2):
                act.wait_ge(s.wqk_made, k + 1)
                act.activation(wqk[:, 4 * k:4 * k + 4, :],
                               p_mb[k][:, 0:4 * C].rearrange("p (h c) -> p h c", c=C), ACT.Copy)\
                    .then_inc(s.wqk_copied, 1)
            act.wait_ge(s.xnT_made, 1)
            act.activation(xnT[:, 0:TOK], p_mb[2][:, 0:TOK], ACT.Copy).then_inc(s.xnT_copied, 1)
            for g in range(G):
                act.wait_ge(s.first_q_made, g + 1)
                act.activation(q_now[0][0:C, g * GQ:(g + 1) * GQ], q_banks[g][0:C, 0:GQ], ACT.Copy)\
                    .then_inc(s.q_copied, 1)
            act.wait_ge(s.xnT_made, 2)
            act.activation(xnT[:, TOK:ALLTOK], p_x[:, TOK:ALLTOK], ACT.Copy).then_inc(s.xnT_copied, 1)
            for h in range(H):
                q_psum = q_banks[h % 4][0:C, S:ALLTOK]
                act.wait_ge(s.q_made, h + 1)
                act.activation(q_hi[:, 1:B, h * S:(h + 1) * S], q_psum.rearrange("p (b i) -> p b i", i=S), ACT.Copy)\
                    .then_inc(s.q_hi_made, 1)
                act.activation(q_full[h], q_psum, ACT.Copy).then_inc(s.q_full_made, 1)
            act.wait_ge(s.q_hi_made, H)
            for k, cols in enumerate((slice(0, 3 * GQ), slice(3 * GQ, HQ))):
                act.wait_ge(s.row_made, k + 1)
                act.activation(q_now[0][C:C + 1, cols], p_x[C:C + 1, cols], ACT.Copy)\
                    .then_inc(max_moved[0], 8 * G)

            def copy_q(b, par):
                act.activation(q_now[par][0:C, :], q_hi[:, bass.ds(b, 1), :].rearrange("c o n -> c (o n)"),
                               ACT.Copy).then_inc(s.q_copied, 1)

            def split_ctx_hi(b, par, half, part):
                if part == 0:
                    act.wait_ge(ctx_loaded[par], 16 * half + 16)
                tiles = slice(part * 3, part * 3 + 3)
                act.activation(ctx_hi[par][:, tiles, 0:C], ctx_in[par][:, tiles, :], ACT.Copy)\
                    .then_inc(s.ctx_hi_made, 1)

            def batch(b, par, half, first, last):
                if not last:
                    copy_q(b + 1, 1 - par)
                for t in range(T):
                    n = T * b + t
                    k = t % RING
                    if first and t in (2, 6):
                        part = t // 4
                        act.wait_ge(s.wvo_made, part + 1)
                        act.activation(wvo[:, 4 * part:4 * part + 4, :],
                                       p_x[0:C, 0:4 * D].rearrange("p (h c) -> p h c", c=D), ACT.Copy)\
                            .then_inc(s.wvo_copied, 1)
                    if not last and t in CTX_STEPS:
                        split_ctx_hi(b + 1, 1 - par, half + par, CTX_STEPS.index(t))
                    act.wait_ge(s.scored, n + 1)
                    if not (first and t < RING):
                        act.wait_ge(s.pv_done, n - RING + 1)
                    act.activation(e_hi[:, k, :], p_s[t % 2][0:KT, 0:HQ], ACT.Exp, scale=SCALE)\
                        .then_inc(s.exp_made, 1)
                    act.activation(e_full[:, k, :], p_s[t % 2][0:KT, 0:HQ], ACT.Exp, scale=SCALE)\
                        .then_inc(s.exp_made, 1)

            batches(act, batch)
            act.activation(warm[:, :], sig127[0:1, :], ACT.Silu).then_inc(s.act_warm, 1)
            act.wait_ge(s.xhT_made, 1)
            act.activation(xhT[:, :], p_s[1][:, 0:ALLTOK], ACT.Copy).then_inc(s.xhT_copied, 1)
            act.wait_ge(s.x1T_made, 1)
            act.activation(x1T[:, :], p_s[0][:, 0:ALLTOK], ACT.Copy).then_inc(s.x1T_copied, 1)
            act.wait_ge(s.xscale_made, 1)
            for f, (f0, fn) in enumerate(FT):
                act.wait_ge(s.gate_made, f + 1)
                act.activation(silu[0:fn, f, :], g_banks[f][0:fn, 0:ALLTOK], ACT.Silu,
                               scale=xscale[0:fn, f:f + 1]).then_inc(s.silu_made, 1)

        @block.vector
        def _(dve):
            dve.memset(warm[:, :], 0.0).then_inc(s.warm_made, 1)
            dve.memset(hmax[:, :], 0.0)
            dve.memset(filler[:, :], 0.0).then_inc(s.filler_made, 1)
            dve.memset(wmax[:, :], 1.0).then_inc(s.w_step, 1)
            dve.wait_ge(s.x_loaded, 16)
            for p in range(PAIRS):
                last = dve.bn_stats(stats[:, p, :], x_in[:, p, :])
            last.then_inc(s.ln_step, 1)
            dve.wait_ge(s.ln_step, 1)
            for p in range(PAIRS):
                last = dve.bn_aggr(mv[:, p, :], stats[:, p, :])
            last.then_inc(s.ln_step, 1)
            dve.wait_ge(s.ln_step, 2)
            dve.tensor_scalar(veps[:, :], mv[:, :, 1], EPS, None, ALU.add).then_inc(s.ln_step, 1)
            dve.wait_ge(s.ln_step, 3)
            dve.wait_ge(s.pow_made, 1)
            newton(dve, rstd[:, :], nt[:, :], veps[:, :], s.ln_step, 3)

            def split_ctxT_hi(b, par, half, first=False):
                dve.wait_ge(ctxT_loaded[par], 16 * half + 16)
                if not first:
                    dve.wait_ge(s.scored, T * (b - 1))
                dve.tensor_copy(ctxT_hi[par][0:C, :], ctxT_in[par][:, :]).then_inc(s.ctxT_hi_made, 1)

            for p in range(PAIRS):
                if p == 1:
                    split_ctxT_hi(0, 0, 0, True)
                dve.tensor_scalar(xn[:, p, :], x_in[:, p, :], mv[:, p, 0:1], rstd[:, p:p + 1],
                                  ALU.subtract, ALU.mult).then_inc(s.xn_made, 1)

            def split_ctxT_lo(b, par):
                dve.wait_ge(s.ctxT_hi_made, b + 1)
                dve.tensor_tensor(ctxT_lo[par][:, :], ctxT_in[par][:, :], ctxT_hi[par][0:C, :], ALU.subtract)\
                    .then_inc(s.ctxT_lo_made, 1)

            def split_ctx_lo(b, par):
                dve.wait_ge(s.ctx_hi_made, 4 * (b + 1))
                dve.tensor_tensor(ctx_lo[par][:, :, :], ctx_in[par][:, :, :], ctx_hi[par][:, :, 0:C],
                                  ALU.subtract).then_inc(s.ctx_lo_made, 1)

            def chunk(b, c):
                dve.wait_ge(s.max_scored, CHUNKS * b + c + 1)
                dve.reduce_max(chunk_max[:, c // NM, c % NM:c % NM + 1], p_mb[c % NM][0:GQ, 0:MC], AX.X)\
                    .then_inc(s.chunk_max_made, 1)

            def group(b, par, g):
                dve.wait_ge(s.chunk_max_made, CHUNKS * b + NM * g + NM)
                dve.reduce_max(maxima[par][:, g:g + 1], chunk_max[:, g, :], AX.X).then_inc(s.max_made, 1)

            for g in range(G):
                dve.wait_ge(s.q_copied, g + 1)
                cols = slice(g * GQ, (g + 1) * GQ)
                dve.tensor_tensor(q_lo[:, 0, cols], q_banks[g][0:C, 0:GQ], q_now[0][0:C, cols], ALU.subtract)\
                    .then_inc(s.first_q_lo_made, 1)
            for c in range(CHUNKS):
                chunk(0, c)
                if c >= NM and c % NM == 0:
                    group(0, 0, c // NM - 1)
            group(0, 0, G - 1)
            split_ctxT_hi(1, 1, 0, True)
            dve.wait_ge(ctx_loaded[0], 16)
            dve.tensor_copy(ctx_hi[0][:, :, 0:C], ctx_in[0][:, :, :]).then_inc(s.ctx_hi_made, 4)

            def normalise(b, par, step):
                done = 5 * b
                if step == 0:
                    dve.wait_ge(s.pv_done, T * b + T)
                    dve.transpose(den_t[:, :], p_o[par][C:128, 0:HQ]).then_inc(s.norm_step, 1)
                elif step == 1:
                    dve.wait_ge(s.norm_step, done + 1)
                    dve.reciprocal(inv_t[0:32, :], den_t[:, :].rearrange("p (k j) -> p k j", j=32)[:, :, 0])\
                        .then_inc(s.norm_step, 1)
                elif step == 2:
                    dve.wait_ge(s.norm_step, done + 2)
                    dve.tensor_copy(inv_t[32:64, :], inv_t[0:32, :]).then_inc(s.norm_step, 1)
                    dve.tensor_copy(inv_t[64:96, :], inv_t[0:32, :]).then_inc(s.norm_step, 1)
                elif step == 3:
                    dve.wait_ge(s.norm_step, done + 4)
                    dve.transpose(inv[:, :], inv_t[:, :].unsqueeze(2).to_broadcast([C, HQ // 32, 32]))\
                        .then_inc(s.norm_step, 1)
                else:
                    dve.wait_ge(s.norm_step, done + 5)
                    dve.tensor_tensor(attn[:, :, par, :], p_o[par][0:C, 0:HQ].rearrange("p (h i) -> p h i", i=S),
                                      inv[:, :].rearrange("p (h i) -> p h i", i=S), ALU.mult)\
                        .then_inc(s.attn_made, 1)

            def normalise_last():
                for step in range(3):
                    normalise(B - 1, 1, step)
                dve.wait_ge(s.norm_step, 5 * (B - 1) + 4)
                halves = [(slice(k * (HQ // 2), (k + 1) * (HQ // 2)), slice(k * (HQ // 64), (k + 1) * (HQ // 64)),
                           slice(k * (H // 2), (k + 1) * (H // 2))) for k in range(2)]
                for cols, blocks, _ in halves:
                    dve.transpose(inv[:, cols], inv_t[:, blocks].unsqueeze(2).to_broadcast([C, HQ // 64, 32]))\
                        .then_inc(s.norm_step, 1)
                for k, (cols, _, heads) in enumerate(halves):
                    dve.wait_ge(s.norm_step, 5 * B + k)
                    dve.tensor_tensor(attn[:, heads, 1, :], p_o[1][0:C, cols].rearrange("p (h i) -> p h i", i=S),
                                      inv[:, cols].rearrange("p (h i) -> p h i", i=S), ALU.mult)\
                        .then_inc(s.last_attn_made, 1)

            def residual(p, step):
                if step == 0:
                    dve.wait_ge(s.projected, p + 1)
                    dve.tensor_tensor(x1_now[:, :], p_x[0:TOK, 0:D],
                                      xb[:, bass.ds(p, 1), :].rearrange("t o n -> t (o n)"), ALU.add)\
                        .then_inc(s.x1_made, 1)
                elif step == 1:
                    dve.wait_ge(s.x1_made, p + 1)
                    dve.bn_stats(stats2[:, :], x1_now[:, :]).then_inc(s.ln2_step, 1)
                elif step == 2:
                    dve.wait_ge(s.ln2_step, 6 * p + 1)
                    dve.tensor_scalar(x1[:, bass.ds(p, 1), :].rearrange("t o n -> t (o n)"), x1_now[:, :],
                                      1.0, None, ALU.mult)
                    dve.bn_aggr(mv2[:, :], stats2[:, :]).then_inc(s.ln2_step, 1)
                else:
                    dve.wait_ge(s.ln2_step, 6 * p + 2)
                    dve.tensor_scalar(veps2[:, :], mv2[:, 1:2], EPS, None, ALU.add).then_inc(s.veps2_made, 1)

            def layernorm2(p):
                dve.wait_ge(s.pow2_made, p + 1)
                newton(dve, rstd2[:, :], nt2[:, :], veps2[:, :], s.ln2_step, 6 * p + 2)
                dve.tensor_scalar(xh[:, bass.ds(p, 1), :].rearrange("t o n -> t (o n)"), x1_now[:, :],
                                  mv2[:, 0:1], rstd2[:, :], ALU.subtract, ALU.mult).then_inc(s.xh_made, 1)

            def quantise_weights():
                dve.wait_ge(s.ffn_loaded, 80)
                for k, w in ((0, wg), (3, wu)):
                    dve.reduce_max(wmax[:, k:k + 2], w[:, 0:2, :], AX.X, apply_absolute_value=True)
                    dve.reduce_max(wmax[0:96, k + 2:k + 3], w[0:96, 2, :], AX.X, apply_absolute_value=True)
                dve.reduce_max(wmax[:, 6:7], wd[:, :], AX.X, apply_absolute_value=True).then_inc(s.w_step, 1)
                dve.wait_ge(s.w_step, 2)
                dve.tensor_scalar(wscale[:, :], wmax[:, :], 1.0 / QMAX, None, ALU.mult).then_inc(s.w_step, 1)
                dve.wait_ge(s.w_step, 3)
                dve.reciprocal(winv[:, :], wscale[:, :]).then_inc(s.w_step, 1)
                dve.wait_ge(s.w_step, 4)
                jobs = [(w[0:fn, f, :], q[0:fn, f, :], winv[0:fn, k + f:k + f + 1], slice((k + f) * D, (k + f + 1) * D))
                        for k, w, q in ((0, wg, wg_q), (3, wu, wu_q)) for f, (_, fn) in enumerate(FT)]
                jobs += [(wd[:, :], wd_q[:, :], winv[:, 6:7], slice(6 * D, 6 * D + F))]
                for w, q, r, cols in jobs:
                    dve.tensor_scalar(wt1[0:w.shape[0], cols], w, r, ROUND, ALU.mult, ALU.add).then_inc(s.w_step, 1)
                for n, (w, q, r, cols) in enumerate(jobs):
                    fn = w.shape[0]
                    dve.wait_ge(s.w_step, 5 + n)
                    dve.tensor_scalar(wt2[0:fn, cols], wt1[0:fn, cols], ROUND, QMAX, ALU.subtract, ALU.min)\
                        .then_inc(s.w_step2, 1)
                for n, (w, q, r, cols) in enumerate(jobs):
                    dve.wait_ge(s.w_step2, 1 + n)
                    dve.tensor_scalar(q, wt2[0:w.shape[0], cols], -QMAX - 1, None, ALU.max)\
                        .then_inc(s.w_quantised, 1)

            def copy_weights():
                src = p_x[:, :].bitcast(BF16)
                for k, dst in enumerate((wgT[:, :], wuT[:, :], wdT[:, :, :])):
                    dve.wait_ge(s.wT_made, k + 1)
                    if k < 2:
                        dve.tensor_copy(dst, src[:, 0:F]).then_inc(s.wT_copied, 1)
                    else:
                        dve.tensor_copy(dst[:, 0:2, :], src[:, 0:2 * D].rearrange("p (f n) -> p f n", n=D))
                        dve.tensor_copy(dst[0:96, 2, :], src[0:96, 2 * D:3 * D]).then_inc(s.wT_copied, 1)

            def batch(b, par, half, first, last):
                nxt, nhalf = b + 1, half + par
                if not last and not first:
                    split_ctxT_hi(nxt, 1 - par, nhalf)
                split_ctx_lo(b, par)
                if first:
                    dve.wait_ge(s.bias_loaded, 48)
                    dve.tensor_tensor(xb[:, :, :], x_in[:, :, :],
                                      bout[:, :].unsqueeze(1).to_broadcast([TOK, PAIRS, D]), ALU.add)
                    dve.wait_ge(s.clip_exp, 1)
                    dve.tensor_scalar(sig127[:, :], sig127[:, :], 1.0, QMAX, ALU.add, ALU.mult)\
                        .then_inc(s.clip_step, 1)
                    dve.wait_ge(s.clip_step, 1)
                    dve.reciprocal(sig127[:, :], sig127[:, :]).then_inc(s.attn_made, 1)
                if last:
                    for step in range(5):
                        normalise(b - 1, 1 - par, step)
                    quantise_weights()
                    copy_weights()
                    return
                for c in range(CHUNKS):
                    chunk(nxt, c)
                    if not first and 2 <= c <= 6:
                        normalise(b - 1, 1 - par, c - 2)
                    if not first and par == 0 and 8 <= c:
                        residual(half - 1, c - 8)
                    if c >= NM and c % NM == 0:
                        group(nxt, 1 - par, c // NM - 1)
                group(nxt, 1 - par, G - 1)
                split_ctxT_lo(nxt, 1 - par)
                if not first and par == 0:
                    layernorm2(half - 1)

            batches(dve, batch)
            dve.reduce_max(xmax[:, 0:3], xh[:, 0:3, :], AX.X, apply_absolute_value=True).then_inc(s.xmax3_step, 1)
            dve.wait_ge(s.xmax3_step, 1)
            dve.reduce_max(xmax[:, 2:3], xmax[:, 0:3], AX.X).then_inc(s.xmax_step, 1)
            normalise_last()
            for step in range(4):
                residual(PAIRS - 1, step)
            dve.wait_ge(s.ln2_step, 6 * PAIRS - 4)
            dve.tensor_scalar(x1_now[:, :], x1_now[:, :], mv2[:, 0:1], None, ALU.subtract).then_inc(s.xmax_step, 1)
            dve.wait_ge(s.xmax_step, 2)
            dve.reduce_max(xmax1[:, :], x1_now[:, :], AX.X, apply_absolute_value=True).then_inc(s.xmax_step, 1)
            dve.wait_ge(s.pow2_made, PAIRS)
            newton(dve, rstd2[:, :], nt2[:, :], veps2[:, :], s.ln2_step, 6 * (PAIRS - 1) + 2)
            dve.tensor_tensor(xmax[:, 3:4], xmax1[:, :], rstd2[:, :], ALU.mult).then_inc(s.xmax_step, 1)
            dve.tensor_scalar(xh[:, PAIRS - 1, :], x1_now[:, :], rstd2[:, :], None, ALU.mult).then_inc(s.xh_made, 1)
            dve.wait_ge(s.xmax_spread, 1)
            dve.reduce_max(xs[:, 0:1], p_mb[0][:, 0:2 * TOK], AX.X).then_inc(s.xmax_step, 1)
            dve.wait_ge(s.xmax_step, 5)
            dve.tensor_scalar(xs[:, 1:2], xs[:, 0:1], sig127[:, 0:1], None, ALU.mult).then_inc(s.xmax_step, 1)
            dve.wait_ge(s.xmax_step, 6)
            dve.reciprocal(xs[:, 2:3], xs[:, 1:2]).then_inc(s.xmax_step, 1)
            dve.tensor_scalar(xscale[:, :], wscale[:, 0:6], xs[:, 1:2], None, ALU.mult).then_inc(s.xscale_made, 1)
            dve.wait_ge(s.xmax_step, 7)
            dve.wait_ge(s.xhT_copied, 1)
            dve.tensor_scalar(xt1[:, :], xhT[:, :], xs[:, 2:3], ROUND, ALU.mult, ALU.add).then_inc(s.xmax_step, 1)
            dve.wait_ge(s.xmax_step, 8)
            dve.tensor_scalar(xt2[:, :], xt1[:, :], ROUND, QMAX, ALU.subtract, ALU.min).then_inc(s.xmax_step, 1)
            dve.wait_ge(s.xmax_step, 9)
            dve.tensor_scalar(xq[:, :], xt2[:, :], -QMAX - 1, None, ALU.max).then_inc(s.x_quantised, 1)
            for f, (_, fn) in enumerate(FT):
                dve.wait_ge(s.up_made, f + 1)
                dve.wait_ge(s.silu_made, f + 1)
                dve.scalar_tensor_tensor(hh[0:fn, f, :], u_banks[f][0:fn, 0:ALLTOK], xscale[0:fn, 3 + f:4 + f],
                                         silu[0:fn, f, :], ALU.mult, ALU.mult).then_inc(s.h_step, 1)
                dve.wait_ge(s.h_step, f + 1)
                last = dve.reduce_max(hmax[0:fn, f:f + 1], hh[0:fn, f, :], AX.X, apply_absolute_value=True)
            last.then_inc(s.h_step, 1)
            dve.wait_ge(s.h_step, 4)
            dve.reduce_max(hmax1[:, :], hmax[:, :], AX.X).then_inc(s.hmax_ready, 1)
            dve.wait_ge(s.hmax_spread, 1)
            dve.reduce_max(hs[:, 0:1], p_o[0][:, 0:128], AX.X).then_inc(s.h_step, 1)
            dve.wait_ge(s.h_step, 5)
            dve.tensor_scalar(hs[:, 1:2], hs[:, 0:1], sig127[:, 1:2], None, ALU.mult).then_inc(s.h_step, 1)
            dve.wait_ge(s.h_step, 6)
            dve.reciprocal(hs[:, 2:3], hs[:, 1:2]).then_inc(s.h_step, 1)
            dve.wait_ge(s.h_step, 7)
            for k, (fn, tiles) in enumerate(((128, slice(0, 2)), (96, slice(2, 3)))):
                dve.tensor_scalar(ht1[0:fn, tiles, :], hh[0:fn, tiles, :], hs[0:fn, 2:3], ROUND, ALU.mult, ALU.add)\
                    .then_inc(s.h_step, 1)
            dve.tensor_tensor(hs[:, 0:1], hs[:, 1:2], wscale[:, 6:7], ALU.mult).then_inc(s.y_step, 1)
            for k, (fn, tiles) in enumerate(((128, slice(0, 2)), (96, slice(2, 3)))):
                dve.wait_ge(s.h_step, 8 + k)
                dve.tensor_scalar(ht2[0:fn, tiles, :], ht1[0:fn, tiles, :], ROUND, QMAX, ALU.subtract, ALU.min)\
                    .then_inc(s.h_step2, 1)
            for k, (fn, tiles) in enumerate(((128, slice(0, 2)), (96, slice(2, 3)))):
                dve.wait_ge(s.h_step2, 1 + k)
                dve.tensor_scalar(hq[0:fn, tiles, :], ht2[0:fn, tiles, :], -QMAX - 1, None, ALU.max)\
                    .then_inc(s.h_quantised, 1)
            dve.wait_ge(s.y_made, 1)
            dve.wait_ge(s.x1T_copied, 1)
            dve.scalar_tensor_tensor(y[:, :], p_o[1][:, 0:ALLTOK], hs[:, 0:1], x1T[:, :], ALU.mult, ALU.add)\
                .then_inc(s.y_step, 1)

        @block.tensor
        def _(pe):
            def busy(n, bank):
                for _ in range(n):
                    pe.matmul(bank[:, :], filler[:, 0:128], filler[:, :], start=True, stop=True)

            pe.wait_ge(s.filler_made, 1)
            busy(10, p_x)
            pe.wait_ge(s.qk_loaded, 32)
            for h in range(H):
                last = pe.matmul(p_mb[h // 4][:, (h % 4) * C:(h % 4 + 1) * C], wqT[:, h, :], wkT[:, h, :],
                                 start=True, stop=True)
                if h % 4 == 3:
                    last.then_inc(s.wqk_made, 1)
            pe.wait_ge(s.ident_made, 2)
            pe.wait_ge(s.xn_made, 1)
            pe.transpose(p_mb[2][:, 0:TOK], xn[:, 0, :], ident[0:TOK, 0:TOK]).then_inc(s.xnT_made, 1)

            def max_chunk(b, par, c, first=False):
                g, k = c // NM, c % NM
                if c == 0:
                    pe.wait_ge(s.ctxT_hi_made, b + 1)
                if first or c == 0:
                    pe.wait_ge(s.q_copied, g + 1 if first else b + G)
                if not (first and c < NM):
                    pe.wait_ge(s.chunk_max_made, CHUNKS * b + c - NM + 1)
                pe.matmul(p_mb[k][0:GQ, 0:MC], q_now[par][0:C, g * GQ:(g + 1) * GQ],
                          ctxT_hi[par][0:C, k * MC:(k + 1) * MC], start=True, stop=True).then_inc(s.max_scored, 1)

            def scores(b, par, half, t, first):
                n = T * b + t
                if t == 0:
                    pe.wait_ge(s.ctxT_lo_made, b + 1)
                    if first:
                        pe.wait_ge(s.first_q_lo_made, G)
                    else:
                        pe.wait_ge(max_moved[par], 16 * G * (half + 1))
                if not (first and t < 2):
                    pe.wait_ge(s.exp_made, 2 * (n - 1))
                keys = slice(t * KT, (t + 1) * KT)
                o = p_s[t % 2][0:KT, 0:HQ]
                pe.matmul(o, ctxT_lo[par][:, keys], q_now[par][0:C, :], start=True, stop=False)
                pe.matmul(o, ctxT_hi[par][0:C, keys], q_lo[:, bass.ds(b, 1), :].rearrange("c o n -> c (o n)"),
                          start=False, stop=False)
                if first and t == 0:
                    pe.wait_ge(max_moved[0], 16 * G)
                pe.matmul(o, ctxT_hi[par][:, keys], q_now[par][:, :], start=False, stop=True).then_inc(s.scored, 1)

            def weighted(b, par, t, early=False):
                n = T * b + t
                k = t % RING
                if t == 0:
                    pe.wait_ge(s.ctx_lo_made, b + 1)
                    if not early:
                        pe.wait_ge(s.attn_made, b)
                pe.wait_ge(s.exp_made, 2 * n + 1)
                pe.matmul(p_o[par][:, 0:HQ], ctx_hi[par][:, t, :], e_hi[:, k, :], start=(t == 0), stop=False,
                          skip_group_check=True)
                pe.matmul(p_o[par][0:C, 0:HQ], ctx_lo[par][:, t, :], e_hi[:, k, :], start=False, stop=False,
                          skip_group_check=True)
                pe.wait_ge(s.lo_made, n + 1)
                pe.matmul(p_o[par][:, 0:HQ], ctx_hi[par][:, t, :], e_lo[:, k, :], start=False, stop=(t == T - 1),
                          skip_group_check=True).then_inc(s.pv_done, 1)

            def project(p, static=False):
                pe.wait_ge(s.attn_made, 2 * p + 3)
                for h in range(H):
                    last = pe.matmul(p_x[0:TOK, 0:D], attn[:, h, :, :].rearrange("c b i -> c (b i)"), wvo[:, h, :],
                                     start=(h == 0), stop=(h == H - 1))
                last.then_inc(s.projected, 1)

            def project_last(p):
                for h in range(H):
                    pe.wait_ge(s.last_attn_made, 1 + h // 4)
                    last = pe.matmul(p_x[0:TOK, 0:D], attn[:, h, :, :].rearrange("c b i -> c (b i)"), wvo[:, h, :],
                                     start=(h == 0), stop=(h == H - 1))
                last.then_inc(s.projected, 1)

            def weights_vo(k):
                if k == 0:
                    pe.wait_ge(s.vo_loaded, 32)
                else:
                    pe.wait_ge(s.wvo_copied, k)
                for j in range(4):
                    last = pe.matmul(p_x[0:C, j * D:(j + 1) * D], wvT[:, 4 * k + j, :], wout[:, 4 * k + j, :],
                                     start=True, stop=True)
                last.then_inc(s.wvo_made, 1)

            def transpose_weights(k):
                if k == 0:
                    pe.wait_ge(s.w_quantised, 7)
                else:
                    pe.wait_ge(s.wT_copied, k)
                o = p_x[:, :].bitcast(BF16)
                for f, (f0, fn) in enumerate(FT):
                    if k < 2:
                        last = pe.transpose(o[:, f0:f0 + fn], (wg_q, wu_q)[k][0:fn, f, :], ident16[0:fn, 0:fn])
                    else:
                        last = pe.transpose(o[0:fn, f * D:(f + 1) * D], wd_q[:, f0:f0 + fn], ident16[:, :])
                last.then_inc(s.wT_made, 1)

            def query(h):
                if h < 4:
                    pe.wait_ge(s.first_q_lo_made, h + 1)
                else:
                    pe.wait_ge(s.q_full_made, h - 3)
                pe.matmul(q_banks[h % 4][0:C, S:ALLTOK], wqk[:, h, :], xnT[:, S:ALLTOK], start=True, stop=True)\
                    .then_inc(s.q_made, 1)

            def row(g):
                return pe.matmul(p_x[C:C + 1, g * GQ:(g + 1) * GQ], maxima[0][:, g:g + 1], ident[0:GQ, 0:GQ],
                                 start=True, stop=True)

            pe.wait_ge(s.xnT_copied, 1)
            pe.wait_ge(s.wqk_copied, 2)
            for h in range(H):
                last = pe.matmul(q_banks[h // 2][0:C, (h % 2) * S:(h % 2 + 1) * S], wqk[:, h, :], xnT[:, 0:S], start=True, stop=True)
                if h % 2:
                    last.then_inc(s.first_q_made, 1)
            for p in range(1, PAIRS):
                pe.wait_ge(s.xn_made, p + 1)
                last = pe.transpose(p_x[:, p * TOK:(p + 1) * TOK], xn[:, p, :], ident[0:TOK, 0:TOK])
            last.then_inc(s.xnT_made, 1)
            for g in range(G):
                for k in range(NM):
                    max_chunk(0, 0, NM * g + k, first=True)
                if g == 0:
                    pe.wait_ge(s.xnT_copied, 2)
                query(2 * g)
                if g == G - 1:
                    pe.wait_ge(s.max_made, G - 1)
                    for k in range(G - 1):
                        last = row(k)
                    last.then_inc(s.row_made, 1)
                query(2 * g + 1)
            pe.wait_ge(s.ones_made, 2)
            pe.wait_ge(max_moved[0], 8 * G)
            pe.wait_ge(s.max_made, G)
            row(G - 1).then_inc(s.row_made, 1)

            def batch(b, par, half, first, last):
                for t in range(T):
                    scores(b, par, half, t, first)
                    if not last and 1 <= t <= 8:
                        for c in range(3 * t // 2 - 1, 3 * (t + 1) // 2 - 1):
                            max_chunk(b + 1, 1 - par, c)
                    if not first and par == 0 and t == 6:
                        project(half - 1)
                    if first and t in (1, 5):
                        weights_vo(t // 4)
                    if last and t in (9, 10, 11):
                        transpose_weights(t - 9)
                    if t >= LAG:
                        weighted(b, par, t - LAG, early=first)
                    elif not first:
                        weighted(b - 1, 1 - par, T - LAG + t)

            batch(0, 0, 0, True, False)
            pe.wait_ge(s.q_lo_made, H)
            pe.wait_ge(s.ones_made, 4)
            with pe.Fori(1, PAIRS) as i:
                batch(2 * i - 1, 1, i - 1, False, False)
                batch(2 * i, 0, i, False, False)
            batch(B - 1, 1, PAIRS - 1, False, True)
            for t in range(T - LAG, T):
                weighted(B - 1, 1, t)
            pe.wait_ge(s.xh_made, PAIRS - 1)
            for p in range(PAIRS - 1):
                pe.transpose(p_s[1][:, p * TOK:(p + 1) * TOK], xh[:, p, :], ident[0:TOK, 0:TOK])
                pe.transpose(p_s[0][:, p * TOK:(p + 1) * TOK], x1[:, p, :], ident[0:TOK, 0:TOK])
            pe.wait_ge(s.xmax_step, 1)
            pe.matmul(p_mb[0][:, 0:TOK], xmax[:, 2:3].to_broadcast([TOK, 128]), ident[0:TOK, 0:TOK],
                      start=True, stop=True)
            project_last(PAIRS - 1)
            pe.wait_ge(s.xmax_step, 4)
            pe.matmul(p_mb[0][:, TOK:2 * TOK], xmax[:, 3:4].to_broadcast([TOK, 128]), ident[0:TOK, 0:TOK],
                      start=True, stop=True).then_inc(s.xmax_spread, 1)
            pe.wait_ge(s.xh_made, PAIRS)
            pe.transpose(p_s[1][:, (PAIRS - 1) * TOK:PAIRS * TOK], xh[:, PAIRS - 1, :], ident[0:TOK, 0:TOK])\
                .then_inc(s.xhT_made, 1)
            pe.transpose(p_s[0][:, (PAIRS - 1) * TOK:PAIRS * TOK], x1[:, PAIRS - 1, :], ident[0:TOK, 0:TOK])\
                .then_inc(s.x1T_made, 1)
            pe.wait_ge(s.x1T_copied, 1)
            pe.wait_ge(s.x_quantised, 1)
            for f, (f0, fn) in enumerate(FT):
                pe.matmul(g_banks[f][0:fn, 0:ALLTOK], wgT[:, f0:f0 + fn], xq[:, :], start=True, stop=True)\
                    .then_inc(s.gate_made, 1)
                pe.matmul(u_banks[f][0:fn, 0:ALLTOK], wuT[:, f0:f0 + fn], xq[:, :], start=True, stop=True)\
                    .then_inc(s.up_made, 1)
            pe.wait_ge(s.hmax_ready, 1)
            pe.matmul(p_o[0][:, 0:128], hmax1[:, 0:1].to_broadcast([128, 128]), ident[:, :],
                      start=True, stop=True).then_inc(s.hmax_spread, 1)
            pe.wait_ge(s.h_quantised, 2)
            for f, (f0, fn) in enumerate(FT):
                last = pe.matmul(p_o[1][:, 0:ALLTOK], wdT[0:fn, f, :], hq[0:fn, f, :], start=(f == 0), stop=(f == 2))
            last.then_inc(s.y_made, 1)


def newton(dve, r, t, v, step, n):
    dve.tensor_tensor(t, r, r, ALU.mult).then_inc(step, 1)
    dve.wait_ge(step, n + 1)
    dve.tensor_tensor(t, t, v, ALU.mult).then_inc(step, 1)
    dve.wait_ge(step, n + 2)
    dve.tensor_scalar(t, t, -0.5, 1.5, ALU.mult, ALU.add).then_inc(step, 1)
    dve.wait_ge(step, n + 3)
    dve.tensor_tensor(r, r, t, ALU.mult).then_inc(step, 1)
    dve.wait_ge(step, n + 4)


def kernel(x, ctx_768, L0_xattn_Wq, L0_xattn_Wk, L0_xattn_Wv, L0_xattn_Wout, L0_xattn_bout,
           L0_ffn_clip_x, L0_ffn_clip_down, L0_ffn_w_gate, L0_ffn_w_up, L0_ffn_w_down):
    import numpy as np
    from concourse import bacc
    from concourse.bass_utils import run_bass_kernel_spmd

    a = {k: np.asarray(v) for k, v in locals().items() if k not in ("np", "bacc", "run_bass_kernel_spmd")}
    ctx = a["ctx_768"]
    arrays = {
        "x_in_d": a["x"].reshape(PAIRS, TOK, D).transpose(1, 0, 2),
        "ctxT_d": ctx.transpose(0, 2, 1),
        "ctx_d": ctx.reshape(B, T, KT, C).transpose(0, 2, 1, 3).reshape(B, KT, T * C),
        "wqT_d": a["L0_xattn_Wq"].reshape(D, H, DH).transpose(2, 1, 0),
        "wkT_d": a["L0_xattn_Wk"].reshape(C, H, DH).transpose(2, 1, 0),
        "wvT_d": a["L0_xattn_Wv"].reshape(C, H, DH).transpose(2, 1, 0),
        "wout_d": a["L0_xattn_Wout"].reshape(H, DH, D).transpose(1, 0, 2),
        "bout_d": np.broadcast_to(a["L0_xattn_bout"][None], (TOK, D)),
        "clipx_d": np.broadcast_to(a["L0_ffn_clip_x"][None], (128, 1)),
        "clipd_d": np.broadcast_to(a["L0_ffn_clip_down"][None], (128, 1)),
        "wg_d": a["L0_ffn_w_gate"], "wu_d": a["L0_ffn_w_up"], "wd_d": a["L0_ffn_w_down"],
    }
    arrays = {k: np.ascontiguousarray(v) for k, v in arrays.items()}
    nc = bacc.Bacc("TRN2", target_bir_lowering=False, num_devices=1)
    args = [nc.dram_tensor(k, v.shape, mybir.dt.from_np(v.dtype), kind="ExternalInput").ap() for k, v in arrays.items()]
    out = nc.dram_tensor("out_d", (D, ALLTOK), F32, kind="ExternalOutput").ap()
    program(nc, *args, out)
    r = run_bass_kernel_spmd(nc, [arrays], core_ids=[0])
    got = r.results[0]["out_d"]
    return got.T.reshape(B, S, D)
```

```python
import concourse.bass as bass
from concourse import mybir
from contextlib import ExitStack

F32 = mybir.dt.float32
F32R = mybir.dt.float32r
BF16 = mybir.dt.bfloat16
ACT = mybir.ActivationFunctionType
ALU = mybir.AluOpType
AX = mybir.AxisListType

B, S, D = 8, 56, 128
M, C = 1500, 96
H, DH = 8, 64
F = 352
KT = 125
T = M // KT
HQ = H * S
G = 4
GQ = HQ // G
MC = 500
NM = M // MC
CHUNKS = G * NM
PAIRS = B // 2
TOK = 2 * S
ALLTOK = B * S
LAG = 3
CTX_STEPS = (4, 6, 7, 9)
CHUNK_PLAN = (0, 2, 1, 2, 1, 2, 1, 2, 1)
FIRST_CHUNK_PLAN = (0, 0, 2, 2, 1, 2, 2, 1, 2)
FIRST_QUERY_PLAN = (1, 2, 2, 3)
DVE_HEADS = 2
RING = 4
SCALE = DH ** -0.5
EPS = 1e-5
QMAX = 127.0
ROUND = 1.5 * 2.0 ** 23
HALVES = [slice(0, ALLTOK // 2), slice(ALLTOK // 2, ALLTOK)]
FT = [(0, 128), (128, 128), (256, 96)]


def program(nc, x_d, ctxT_d, ctx_d, wqT_d, wkT_d, wvT_d, wout_d, bout_d, clipx_d, clipd_d,
            wg_d, wu_d, wd_d, out_d):
    stack = ExitStack()
    with stack:
        def sb(name, shape, dt=F32):
            return stack.enter_context(nc.sbuf_tensor(name, shape, dt))

        def ps(name, cols=512, dt=F32):
            return stack.enter_context(nc.psum_tensor(name, [128, cols], dt))

        def sem(name):
            return stack.enter_context(nc.semaphore(name))

        ident = sb("ident", [128, 128])
        ident16 = sb("ident16", [128, 128], BF16)
        wqT, wkT = sb("wqT", [DH, H, D]), sb("wkT", [DH, H, C])
        wvT, wout = sb("wvT", [DH, H, C]), sb("wout", [DH, H, D])
        wqk = sb("wqk", [D, H, C])
        wvo = sb("wvo", [C, H, D])
        bout = sb("bout", [TOK, D])
        clips = sb("clips", [128, 2])
        sig127 = sb("sig127", [128, 2])
        x_in = sb("x_in", [TOK, PAIRS, D])
        xb = sb("xb", [TOK, PAIRS, D])
        stats = sb("stats", [TOK, PAIRS, 6])
        mv = sb("mv", [TOK, PAIRS, 2])
        rstd = sb("rstd", [TOK, PAIRS])
        veps = sb("veps", [TOK, PAIRS])
        nt = sb("nt", [TOK, PAIRS])
        minus_half = sb("minus_half", [TOK, PAIRS])
        xn = sb("xn", [TOK, PAIRS, D])
        xnT = sb("xnT", [D, ALLTOK])
        x1_now = sb("x1_now", [TOK, D])
        x1 = sb("x1", [TOK, PAIRS, D])
        xh = sb("xh", [TOK, PAIRS, D])
        stats2, mv2 = sb("stats2", [TOK, 6]), sb("mv2", [TOK, 2])
        veps2, rstd2, nt2 = sb("veps2", [TOK, 1]), sb("rstd2", [TOK, 1]), sb("nt2", [TOK, 1])
        q_hi = sb("q_hi", [C, B, HQ], F32R)
        q_lo = sb("q_lo", [C, B, HQ], F32R)
        q_now = [sb(f"q_now{p}", [C + 1, HQ], F32R) for p in range(2)]
        ctxT_in = [sb(f"ctxT_in{p}", [C, M]) for p in range(2)]
        ctxT_hi = [sb(f"ctxT_hi{p}", [C + 1, M], F32R) for p in range(2)]
        ctxT_lo = [sb(f"ctxT_lo{p}", [C, M], F32R) for p in range(2)]
        ctx_in = [sb(f"ctx_in{p}", [KT, T, C]) for p in range(2)]
        ctx_hi = [sb(f"ctx_hi{p}", [KT, T, D], F32R) for p in range(2)]
        ctx_lo = [sb(f"ctx_lo{p}", [KT, T, C], F32R) for p in range(2)]
        chunk_max = sb("chunk_max", [GQ, G, NM])
        maxima = [sb(f"maxima{p}", [GQ, G]) for p in range(2)]
        e_full = sb("e_full", [KT, RING, HQ])
        e_hi = sb("e_hi", [KT, RING, HQ], F32R)
        e_lo = sb("e_lo", [KT, RING, HQ], F32R)
        den_t = sb("den_t", [32, HQ])
        inv_t = sb("inv_t", [C, HQ // 32])
        inv = sb("inv", [C, HQ])
        attn = sb("attn", [C, H, 2, S])
        wg, wu = sb("wg", [128, 3, D]), sb("wu", [128, 3, D])
        wd = sb("wd", [D, F])
        wg_q, wu_q = sb("wg_q", [128, 3, D], BF16), sb("wu_q", [128, 3, D], BF16)
        wd_q = sb("wd_q", [D, F], BF16)
        wt1 = sb("wt1", [128, 6 * D + F])
        wt2 = sb("wt2", [128, 6 * D + F], BF16)
        wgT, wuT = sb("wgT", [D, F], BF16), sb("wuT", [D, F], BF16)
        wdT = sb("wdT", [128, 3, D], BF16)
        wmax = sb("wmax", [128, 7])
        wscale, winv = sb("wscale", [128, 7]), sb("winv", [128, 7])
        xmax = sb("xmax", [TOK, PAIRS])
        xmax1 = sb("xmax1", [TOK, 1])
        xs = sb("xs", [128, 3])
        xscale = sb("xscale", [128, 6])
        rounding = sb("rounding", [128, 2])
        xt1, xt2 = sb("xt1", [D, ALLTOK]), sb("xt2", [D, ALLTOK], BF16)
        xq = sb("xq", [D, ALLTOK], BF16)
        silu = sb("silu", [128, 3, ALLTOK])
        up2 = sb("up2", [96, ALLTOK])
        hh = sb("hh", [128, 3, ALLTOK])
        hmax = sb("hmax", [128, 4])
        hmax1 = sb("hmax1", [128, 1])
        hs = sb("hs", [128, 3])
        ht1, ht2 = sb("ht1", [128, 3, ALLTOK]), sb("ht2", [128, 3, ALLTOK], BF16)
        hq = sb("hq", [128, 3, ALLTOK], BF16)
        x1T, y = sb("x1T", [D, ALLTOK]), sb("y", [D, ALLTOK])
        warm = sb("warm", [1, 2])
        filler = sb("filler", [128, 1], BF16)

        q_full = [buf[0:C, j, S:ALLTOK] for buf in (silu, hh, ht1) for j in range(3)]

        p_s = [ps(f"p_s{i}") for i in range(2)]
        p_m = ps("p_m", NM * 512)
        p_o = [ps(f"p_o{i}") for i in range(2)]
        p_x = ps("p_x")

        p_mb = [p_m[:, 512 * i:512 * i + 512] for i in range(NM)]
        q_banks = [p_s[0], p_s[1], p_o[0], p_o[1]]
        g_banks = [p_s[0], p_s[1], p_x]
        u_banks = p_mb
        xh_banks = [p_o[0], p_s[1]]
        y_banks = [p_o[0], p_o[1]]

        names = """
            x_loaded qk_loaded vo_loaded bias_loaded ffn_loaded filler_made warm_made ident_made consts_made ones_made
            ln_step pow_made xn_made xnT_made xnT_copied wqk_made wqk_copied wvo_made wvo_copied clip_exp clip_step
            first_q_made q_copied first_q_full_made first_q_lo_made q_made q_hi_made q_full_made q_lo_made
            last_q_lo_made row_made ctxT_hi_made ctxT_lo_made ctx_hi_made ctx_lo_made
            max_scored chunk_max_made max_made scored exp_made lo_made pv_done norm_step attn_made last_attn_made
            projected x1_made x1_kept ln2_step veps2_made pow2_made x_centred xh_made
            w_step w_step2 w_quantised wT_made wT_copied
            xhT_made x1T_made x1T_copied xmax3_step xmax_step xmax_spread xscale_made x_raised x_quantised
            gate_made up_made up2_made silu_made h_made last_h_made h_step hmax_ready hmax_spread hs_made
            h_step2 h_raised h_quantised y_made y_step out_stored""".split()
        sems = {n: sem(n) for n in names}
        s = type("Sems", (), sems)
        ctxT_loaded = [sem(f"ctxT_loaded{p}") for p in range(2)]
        ctx_loaded = [sem(f"ctx_loaded{p}") for p in range(2)]
        norm_half = [sem(f"norm_half{k}") for k in range(2)]
        max_moved = [sem(f"max_moved{p}") for p in range(2)]

        block = stack.enter_context(nc.Block())

        def batches(eng, batch):
            batch(0, 0, 0, True, False)
            with eng.Fori(1, PAIRS) as i:
                batch(2 * i - 1, 1, i - 1, False, False)
                batch(2 * i, 0, i, False, False)
            batch(B - 1, 1, PAIRS - 1, False, True)

        @block.sync
        def _(sp):
            def load_ctx(b, par, half):
                sp.dma_start(ctxT_in[par][:, :], ctxT_d[bass.ds(b, 1), :, :].rearrange("o c m -> (o c) m"))\
                    .then_inc(ctxT_loaded[par], 16)
                sp.dma_start(ctx_in[par][:, :, :].rearrange("k t c -> k (t c)"),
                             ctx_d[bass.ds(b, 1), :, :].rearrange("o k n -> (o k) n"))\
                    .then_inc(ctx_loaded[par], 16)

            def move_max(b, par):
                for g in range(G):
                    sp.wait_ge(s.max_made, G * b + g + 1)
                    sp.dma_start(q_now[par][C:C + 1, g * GQ:(g + 1) * GQ].bitcast(F32),
                                 maxima[par][:, g:g + 1]).then_inc(max_moved[par], 16)

            sp.dma_start(x_in[:, :, :], x_d).then_inc(s.x_loaded, 16)
            sp.dma_start(wqT[:, :, :], wqT_d).then_inc(s.qk_loaded, 16)
            load_ctx(0, 0, 0)
            sp.wait_ge(s.qk_loaded, 32)
            load_ctx(1, 1, 0)
            sp.dma_start(wg[:, 0:2, :], wg_d[0:256, :].rearrange("(t p) h -> p t h", p=128)).then_inc(s.ffn_loaded, 16)
            sp.dma_start(wg[0:96, 2, :], wg_d[256:F, :]).then_inc(s.ffn_loaded, 16)
            sp.dma_start(wu[:, 0:2, :], wu_d[0:256, :].rearrange("(t p) h -> p t h", p=128)).then_inc(s.ffn_loaded, 16)
            sp.dma_start(wu[0:96, 2, :], wu_d[256:F, :]).then_inc(s.ffn_loaded, 16)
            sp.dma_start(wd[:, :], wd_d).then_inc(s.ffn_loaded, 16)

            def load_second_next(b, par, half):
                sp.wait_ge(s.ctxT_lo_made, b + 1)
                sp.wait_ge(s.ctx_lo_made, b + 1)
                load_ctx(b + 2, par, half)

            load_second_next(0, 0, 0)
            move_max(1, 1)
            with sp.Fori(1, PAIRS - 1) as i:
                load_second_next(2 * i - 1, 1, i)
                move_max(2 * i, 0)
                load_second_next(2 * i, 0, i)
                move_max(2 * i + 1, 1)
            load_second_next(B - 3, 1, 0)
            move_max(B - 2, 0)
            move_max(B - 1, 1)
            sp.wait_ge(s.y_step, 2)
            sp.dma_start(out_d[:, HALVES[0]], y[:, HALVES[0]]).then_inc(s.out_stored, 16)
            sp.wait_ge(s.out_stored, 32)

        @block.gpsimd
        def _(pool):
            pool.memset(ident[:, :], 0.0).then_inc(s.ident_made, 1)
            pool.wait_ge(s.ident_made, 1)
            pool.memset(minus_half[:, :], -0.5).then_inc(s.consts_made, 1)
            pool.wait_ge(s.consts_made, 1)
            pool.affine_select(out=ident[:, :], in_=ident[:, :], compare_op=ALU.not_equal, fill=1.0,
                               base=0, pattern=[[-1, 128]], channel_multiplier=1).then_inc(s.ident_made, 1)
            pool.wait_ge(s.ident_made, 2)
            pool.tensor_copy(ident16[:, :], ident[:, :]).then_inc(s.ident_made, 1)
            pool.wait_ge(s.ident_made, 3)

            def ones(p):
                pool.memset(ctxT_hi[p][C:C + 1, :].bitcast(F32), -1.0).then_inc(s.ones_made, 1)
                pool.wait_ge(s.ones_made, 2 * p + 1)
                pool.memset(ctx_hi[p][:, :, C:D].bitcast(F32), 1.0).then_inc(s.ones_made, 1)
                pool.wait_ge(s.ones_made, 2 * p + 2)

            ones(0)
            pool.wait_ge(s.ln_step, 3)
            pool.tensor_tensor(rstd[:, :], veps[:, :], minus_half[:, :], ALU.pow).then_inc(s.pow_made, 1)
            pool.wait_ge(s.pow_made, 1)
            ones(1)
            pool.wait_ge(s.ctxT_hi_made, 1)
            pool.tensor_tensor(ctxT_lo[0][:, :], ctxT_in[0][:, :], ctxT_hi[0][0:C, :], ALU.subtract)\
                .then_inc(s.ctxT_lo_made, 1)
            pool.wait_ge(s.first_q_full_made, G)
            pool.tensor_tensor(q_lo[:, 0, :], e_full[0:C, 0, :], q_now[0][0:C, :], ALU.subtract)\
                .then_inc(s.first_q_lo_made, 1)
            for h in range(H - DVE_HEADS):
                pool.wait_ge(s.q_full_made, h + 1)
                pool.tensor_tensor(q_lo[:, 1:B, h * S:(h + 1) * S],
                                   q_full[h].rearrange("p (b i) -> p b i", i=S),
                                   q_hi[:, 1:B, h * S:(h + 1) * S], ALU.subtract).then_inc(s.q_lo_made, 1)

            def batch(b, par, half, first, last):
                for t in range(T):
                    n = T * b + t
                    k = t % RING
                    pool.wait_ge(s.exp_made, 2 * n + 2)
                    pool.tensor_tensor(e_lo[:, k, :], e_full[:, k, :], e_hi[:, k, :], ALU.subtract)\
                        .then_inc(s.lo_made, 1)
                    if not first and not last and par == 0 and t == 8:
                        pool.wait_ge(s.veps2_made, half)
                        pool.tensor_tensor(rstd2[:, :], veps2[:, :], minus_half[:, 0:1], ALU.pow)\
                            .then_inc(s.pow2_made, 1)

            batches(pool, batch)
            pool.wait_ge(s.veps2_made, PAIRS)
            pool.tensor_tensor(rstd2[:, :], veps2[:, :], minus_half[:, 0:1], ALU.pow).then_inc(s.pow2_made, 1)
            pool.wait_ge(s.silu_made, 3)
            pool.wait_ge(s.up2_made, 1)
            for cols in HALVES:
                pool.tensor_tensor(hh[0:96, 2, cols], silu[0:96, 2, cols], up2[:, cols], ALU.mult)\
                    .then_inc(s.last_h_made, 1)

        @block.scalar
        def _(act):
            act.wait_ge(s.warm_made, 1)
            act.activation(warm[:, :], warm[:, :], ACT.Exp)
            act.dma_start(wkT[:, :, :], wkT_d).then_inc(s.qk_loaded, 16)
            act.dma_start(clips[:, 0:1], clipx_d).then_inc(s.bias_loaded, 16)
            act.dma_start(clips[:, 1:2], clipd_d).then_inc(s.bias_loaded, 16)
            act.dma_start(bout[:, :], bout_d).then_inc(s.bias_loaded, 16)
            act.dma_start(wvT[:, :, :], wvT_d).then_inc(s.vo_loaded, 16)
            act.dma_start(wout[:, :, :], wout_d).then_inc(s.vo_loaded, 16)
            for k in range(2):
                act.wait_ge(s.wqk_made, k + 1)
                act.activation(wqk[:, 4 * k:4 * k + 4, :],
                               p_mb[k][:, 0:4 * C].rearrange("p (h c) -> p h c", c=C), ACT.Copy)\
                    .then_inc(s.wqk_copied, 1)
                if k == 0:
                    act.wait_ge(s.xnT_made, 1)
                    act.activation(xnT[:, 0:TOK], p_mb[2][:, 0:TOK], ACT.Copy, scale=-0.5).then_inc(s.xnT_copied, 1)
            for g in range(G):
                act.wait_ge(s.first_q_made, g + 1)
                act.activation(q_now[0][0:C, g * GQ:(g + 1) * GQ], q_banks[g][0:C, 0:GQ], ACT.Copy)\
                    .then_inc(s.q_copied, 1)
            act.wait_ge(s.xnT_made, 2)
            act.activation(xnT[:, TOK:ALLTOK], p_x[:, TOK:ALLTOK], ACT.Copy, scale=-0.5).then_inc(s.xnT_copied, 1)
            for g in range(G):
                act.activation(e_full[0:C, 0, g * GQ:(g + 1) * GQ], q_banks[g][0:C, 0:GQ], ACT.Copy)\
                    .then_inc(s.first_q_full_made, 1)
            act.wait_ge(s.bias_loaded, 48)
            act.activation(sig127[:, :], clips[:, :], ACT.Exp, scale=-1.0).then_inc(s.clip_exp, 1)
            def row_copy(k, cols):
                act.wait_ge(s.row_made, k + 1)
                act.activation(q_now[0][C:C + 1, cols], p_x[C:C + 1, cols], ACT.Copy)\
                    .then_inc(max_moved[0], 8 * G)

            for h in range(H):
                q_psum = q_banks[h % 4][0:C, S:ALLTOK]
                if h == H - DVE_HEADS - 1:
                    row_copy(0, slice(0, 3 * GQ))
                if h == H - DVE_HEADS:
                    row_copy(1, slice(3 * GQ, HQ))
                act.wait_ge(s.q_made, h + 1)
                act.activation(q_hi[:, 1:B, h * S:(h + 1) * S], q_psum.rearrange("p (b i) -> p b i", i=S), ACT.Copy)\
                    .then_inc(s.q_hi_made, 1)
                if h < H - DVE_HEADS:
                    act.activation(q_full[h], q_psum, ACT.Copy).then_inc(s.q_full_made, 1)
            act.wait_ge(s.q_hi_made, H)

            def copy_q(b, par):
                act.activation(q_now[par][0:C, :], q_hi[:, bass.ds(b, 1), :].rearrange("c o n -> c (o n)"),
                               ACT.Copy).then_inc(s.q_copied, 1)

            def split_ctx_hi(b, par, half, part):
                if part == 0:
                    act.wait_ge(ctx_loaded[par], 16 * half + 16)
                tiles = slice(part * 3, part * 3 + 3)
                act.activation(ctx_hi[par][:, tiles, 0:C], ctx_in[par][:, tiles, :], ACT.Copy)\
                    .then_inc(s.ctx_hi_made, 1)

            def batch(b, par, half, first, last):
                if not last and not first:
                    copy_q(b + 1, 1 - par)
                for t in range(T):
                    n = T * b + t
                    k = t % RING
                    if first and t == 1:
                        copy_q(b + 1, 1 - par)
                    if first and t in (2, 6):
                        part = t // 4
                        act.wait_ge(s.wvo_made, part + 1)
                        act.activation(wvo[:, 4 * part:4 * part + 4, :],
                                       p_x[0:C, 0:4 * D].rearrange("p (h c) -> p h c", c=D), ACT.Copy)\
                            .then_inc(s.wvo_copied, 1)
                    if not last and t in CTX_STEPS:
                        split_ctx_hi(b + 1, 1 - par, half + par, CTX_STEPS.index(t))
                    act.wait_ge(s.scored, n + 1)
                    if not (first and t < RING):
                        act.wait_ge(s.pv_done, n - RING + 1)
                    act.activation(e_hi[:, k, :], p_s[t % 2][0:KT, 0:HQ], ACT.Exp, scale=SCALE)\
                        .then_inc(s.exp_made, 1)
                    act.activation(e_full[:, k, :], p_s[t % 2][0:KT, 0:HQ], ACT.Exp, scale=SCALE)\
                        .then_inc(s.exp_made, 1)

            batches(act, batch)
            for k, dst in enumerate((wgT[:, :], wuT[:, :], wdT[:, :, :])):
                src = p_mb[k].bitcast(BF16)
                act.wait_ge(s.wT_made, k + 1)
                if k < 2:
                    act.activation(dst, src[:, 0:F], ACT.Copy).then_inc(s.wT_copied, 1)
                else:
                    act.activation(dst[:, 0:2, :], src[:, 0:2 * D].rearrange("p (f n) -> p f n", n=D), ACT.Copy)
                    act.activation(dst[0:96, 2, :], src[0:96, 2 * D:3 * D], ACT.Copy).then_inc(s.wT_copied, 1)
            act.activation(warm[:, :], sig127[0:1, :], ACT.Silu)
            act.wait_ge(s.x1T_made, 1)
            act.activation(x1T[:, :], p_s[0][:, 0:ALLTOK], ACT.Copy).then_inc(s.x1T_copied, 1)

            def raised(t1, t2, src, scale, count):
                act.activation(t1, src, ACT.Identity, bias=rounding[0:src.shape[0], 0:1], scale=scale)\
                    .then_inc(count, 1)
                act.wait_ge(count, 1)
                act.activation(t2, t1, ACT.Relu, bias=rounding[0:src.shape[0], 1:2]).then_inc(count, 1)

            act.wait_ge(s.xmax_step, 7)
            others = HALVES[1]
            raised(xt1[:, others], xt2[:, others], xh_banks[1][:, others], xs[:, 2:3], s.x_raised)
            act.wait_ge(s.xscale_made, 1)
            for f, (f0, fn) in enumerate(FT):
                act.wait_ge(s.gate_made, f + 1)
                act.activation(silu[0:fn, f, :], g_banks[f][0:fn, 0:ALLTOK], ACT.Silu,
                               scale=xscale[0:fn, f:f + 1]).then_inc(s.silu_made, 1)
            act.wait_ge(s.up_made, 3)
            act.activation(up2[:, :], u_banks[2][0:96, 0:ALLTOK], ACT.Identity, scale=xscale[0:96, 5:6])\
                .then_inc(s.up2_made, 1)
            act.wait_ge(s.h_made, 2)
            act.wait_ge(s.hs_made, 1)
            raised(ht1[:, 1, :], ht2[:, 1, :], hh[:, 1, :], hs[:, 2:3], s.h_raised)
            act.wait_ge(s.y_step, 3)
            act.dma_start(out_d[:, HALVES[1]], y[:, HALVES[1]]).then_inc(s.out_stored, 16)

        @block.vector
        def _(dve):
            dve.memset(filler[:, :], 0.0).then_inc(s.filler_made, 1)
            dve.memset(warm[:, :], 0.0).then_inc(s.warm_made, 1)
            dve.memset(hmax[:, :], 0.0)
            dve.memset(rounding[:, 0:1], ROUND)
            dve.memset(rounding[:, 1:2], QMAX + 1 - ROUND)
            dve.memset(wmax[:, :], 1.0).then_inc(s.w_step, 1)
            dve.wait_ge(s.x_loaded, 16)
            for p in range(PAIRS):
                last = dve.bn_stats(stats[:, p, :], x_in[:, p, :])
            last.then_inc(s.ln_step, 1)
            dve.wait_ge(s.ln_step, 1)
            for p in range(PAIRS):
                last = dve.bn_aggr(mv[:, p, :], stats[:, p, :])
            last.then_inc(s.ln_step, 1)
            dve.wait_ge(s.ln_step, 2)
            dve.tensor_scalar(veps[:, :], mv[:, :, 1], EPS, None, ALU.add).then_inc(s.ln_step, 1)
            dve.wait_ge(s.ln_step, 3)
            dve.wait_ge(s.pow_made, 1)
            newton(dve, rstd[:, :], nt[:, :], veps[:, :], s.ln_step, 3)

            def split_ctxT_hi(b, par, half, first=False):
                dve.wait_ge(ctxT_loaded[par], 16 * half + 16)
                if not first:
                    dve.wait_ge(s.scored, T * (b - 1))
                dve.tensor_copy(ctxT_hi[par][0:C, :], ctxT_in[par][:, :]).then_inc(s.ctxT_hi_made, 1)

            for p in range(PAIRS):
                if p == 1:
                    split_ctxT_hi(0, 0, 0, True)
                dve.tensor_scalar(xn[:, p, :], x_in[:, p, :], mv[:, p, 0:1], rstd[:, p:p + 1],
                                  ALU.subtract, ALU.mult).then_inc(s.xn_made, 1)

            def split_ctxT_lo(b, par):
                dve.wait_ge(s.ctxT_hi_made, b + 1)
                dve.tensor_tensor(ctxT_lo[par][:, :], ctxT_in[par][:, :], ctxT_hi[par][0:C, :], ALU.subtract)\
                    .then_inc(s.ctxT_lo_made, 1)

            def split_ctx_lo(b, par):
                dve.wait_ge(s.ctx_hi_made, 4 * (b + 1))
                dve.tensor_tensor(ctx_lo[par][:, :, :], ctx_in[par][:, :, :], ctx_hi[par][:, :, 0:C],
                                  ALU.subtract).then_inc(s.ctx_lo_made, 1)

            def chunk(b, c):
                dve.wait_ge(s.max_scored, CHUNKS * b + c + 1)
                dve.reduce_max(chunk_max[:, c // NM, c % NM:c % NM + 1], p_mb[c % NM][0:GQ, 0:MC], AX.X)\
                    .then_inc(s.chunk_max_made, 1)

            def group(b, par, g):
                dve.wait_ge(s.chunk_max_made, CHUNKS * b + NM * g + NM)
                dve.reduce_max(maxima[par][:, g:g + 1], chunk_max[:, g, :], AX.X).then_inc(s.max_made, 1)

            for c in range(CHUNKS):
                chunk(0, c)
                if c >= NM and c % NM == 0:
                    group(0, 0, c // NM - 1)
            group(0, 0, G - 1)
            split_ctxT_hi(1, 1, 0, True)
            dve.wait_ge(ctx_loaded[0], 16)
            dve.tensor_copy(ctx_hi[0][:, :, 0:C], ctx_in[0][:, :, :]).then_inc(s.ctx_hi_made, 4)
            for h in range(H - DVE_HEADS, H):
                dve.wait_ge(s.q_hi_made, h + 1)
                heads_q = slice(h * S, (h + 1) * S)
                dve.tensor_tensor(q_lo[:, 1:B, heads_q],
                                  q_banks[h % 4][0:C, S:ALLTOK].rearrange("p (b i) -> p b i", i=S),
                                  q_hi[:, 1:B, heads_q], ALU.subtract).then_inc(s.last_q_lo_made, 1)

            def normalise(b, par, step):
                done = 5 * b
                if step == 0:
                    dve.wait_ge(s.pv_done, T * b + T)
                    dve.transpose(den_t[:, :], p_o[par][C:128, 0:HQ]).then_inc(s.norm_step, 1)
                elif step == 1:
                    dve.wait_ge(s.norm_step, done + 1)
                    dve.reciprocal(inv_t[0:32, :], den_t[:, :].rearrange("p (k j) -> p k j", j=32)[:, :, 0])\
                        .then_inc(s.norm_step, 1)
                elif step == 2:
                    dve.wait_ge(s.norm_step, done + 2)
                    dve.tensor_copy(inv_t[32:64, :], inv_t[0:32, :]).then_inc(s.norm_step, 1)
                    dve.tensor_copy(inv_t[64:96, :], inv_t[0:32, :]).then_inc(s.norm_step, 1)
                elif step == 3:
                    dve.wait_ge(s.norm_step, done + 4)
                    dve.transpose(inv[:, :], inv_t[:, :].unsqueeze(2).to_broadcast([C, HQ // 32, 32]))\
                        .then_inc(s.norm_step, 1)
                else:
                    dve.wait_ge(s.norm_step, done + 5)
                    dve.tensor_tensor(attn[:, :, par, :], p_o[par][0:C, 0:HQ].rearrange("p (h i) -> p h i", i=S),
                                      inv[:, :].rearrange("p (h i) -> p h i", i=S), ALU.mult)\
                        .then_inc(s.attn_made, 1)

            def normalise_last():
                step = norm_half
                n_blocks = HQ // 64
                halves = [(k, slice(k * (HQ // 2), (k + 1) * (HQ // 2)), slice(k * n_blocks, (k + 1) * n_blocks),
                           slice(k * (H // 2), (k + 1) * (H // 2))) for k in range(2)]

                def columns(k, cols, blocks, heads):
                    dve.transpose(den_t[:, cols], p_o[1][C:128, cols]).then_inc(step[k], 1)

                def invert(k, cols, blocks, heads):
                    dve.wait_ge(step[k], 1)
                    dve.reciprocal(inv_t[0:32, blocks], den_t[:, cols].rearrange("p (k j) -> p k j", j=32)[:, :, 0])\
                        .then_inc(step[k], 1)

                def spread(k, cols, blocks, heads):
                    dve.wait_ge(step[k], 2)
                    dve.tensor_copy(inv_t[32:64, blocks], inv_t[0:32, blocks]).then_inc(step[k], 1)
                    dve.tensor_copy(inv_t[64:96, blocks], inv_t[0:32, blocks]).then_inc(step[k], 1)

                def rows(k, cols, blocks, heads):
                    dve.wait_ge(step[k], 4)
                    dve.transpose(inv[:, cols], inv_t[:, blocks].unsqueeze(2).to_broadcast([C, n_blocks, 32]))\
                        .then_inc(step[k], 1)

                def scale(k, cols, blocks, heads):
                    dve.wait_ge(step[k], 5)
                    dve.tensor_tensor(attn[:, heads, 1, :], p_o[1][0:C, cols].rearrange("p (h i) -> p h i", i=S),
                                      inv[:, cols].rearrange("p (h i) -> p h i", i=S), ALU.mult)\
                        .then_inc(s.last_attn_made, 1)

                dve.wait_ge(s.pv_done, T * B)
                columns(*halves[0])
                invert(*halves[0])
                columns(*halves[1])
                spread(*halves[0])
                invert(*halves[1])
                rows(*halves[0])
                scale(*halves[0])
                spread(*halves[1])
                rows(*halves[1])
                scale(*halves[1])

            def residual(p, step, last=False):
                if step == 0:
                    dve.wait_ge(s.projected, p + 1)
                    dve.tensor_tensor(x1_now[:, :], p_x[0:TOK, 0:D],
                                      xb[:, bass.ds(p, 1), :].rearrange("t o n -> t (o n)"), ALU.add)\
                        .then_inc(s.x1_made, 1)
                elif step == 1:
                    dve.wait_ge(s.x1_made, p + 1)
                    dve.bn_stats(stats2[:, :], x1_now[:, :]).then_inc(s.ln2_step, 1)
                elif step == 2:
                    dve.wait_ge(s.ln2_step, 5 * p + 1)
                    if not last:
                        dve.tensor_scalar(x1[:, bass.ds(p, 1), :].rearrange("t o n -> t (o n)"), x1_now[:, :],
                                          1.0, None, ALU.mult).then_inc(s.x1_kept, 1)
                    dve.bn_aggr(mv2[:, :], stats2[:, :]).then_inc(s.ln2_step, 1)
                    if last:
                        dve.tensor_copy(x1[:, PAIRS - 1, :], x1_now[:, :]).then_inc(s.x1_kept, 1)
                else:
                    dve.wait_ge(s.ln2_step, 5 * p + 2)
                    dve.tensor_scalar(veps2[:, :], mv2[:, 1:2], EPS, None, ALU.add).then_inc(s.veps2_made, 1)

            def layernorm2(p):
                dve.tensor_scalar(x1_now[:, :], x1_now[:, :], mv2[:, 0:1], None, ALU.subtract)\
                    .then_inc(s.x_centred, 1)
                dve.wait_ge(s.pow2_made, p + 1)
                newton(dve, rstd2[:, :], nt2[:, :], veps2[:, :], s.ln2_step, 5 * p + 2)
                dve.wait_ge(s.x_centred, p + 1)
                dve.tensor_scalar(xh[:, bass.ds(p, 1), :].rearrange("t o n -> t (o n)"), x1_now[:, :],
                                  rstd2[:, :], -0.5, ALU.mult, ALU.mult).then_inc(s.xh_made, 1)

            def quantise_weights():
                dve.wait_ge(s.ffn_loaded, 80)
                for k, w in ((0, wg), (3, wu)):
                    dve.reduce_max(wmax[:, k:k + 2], w[:, 0:2, :], AX.X, apply_absolute_value=True)
                    dve.reduce_max(wmax[0:96, k + 2:k + 3], w[0:96, 2, :], AX.X, apply_absolute_value=True)
                dve.reduce_max(wmax[:, 6:7], wd[:, :], AX.X, apply_absolute_value=True).then_inc(s.w_step, 1)
                dve.wait_ge(s.w_step, 2)
                dve.tensor_scalar(wscale[:, :], wmax[:, :], 1.0 / QMAX, None, ALU.mult).then_inc(s.w_step, 1)
                dve.wait_ge(s.w_step, 3)
                dve.reciprocal(winv[:, :], wscale[:, :]).then_inc(s.w_step, 1)
                dve.wait_ge(s.w_step, 4)
                jobs = [(w[0:fn, f, :], q[0:fn, f, :], winv[0:fn, k + f:k + f + 1], slice((k + f) * D, (k + f + 1) * D))
                        for k, w, q in ((0, wg, wg_q), (3, wu, wu_q)) for f, (_, fn) in enumerate(FT)]
                jobs += [(wd[:, :], wd_q[:, :], winv[:, 6:7], slice(6 * D, 6 * D + F))]
                for w, q, r, cols in jobs:
                    dve.tensor_scalar(wt1[0:w.shape[0], cols], w, r, ROUND, ALU.mult, ALU.add).then_inc(s.w_step, 1)
                for n, (w, q, r, cols) in enumerate(jobs):
                    fn = w.shape[0]
                    dve.wait_ge(s.w_step, 5 + n)
                    dve.tensor_scalar(wt2[0:fn, cols], wt1[0:fn, cols], ROUND, QMAX, ALU.subtract, ALU.min)\
                        .then_inc(s.w_step2, 1)
                for n, (w, q, r, cols) in enumerate(jobs):
                    dve.wait_ge(s.w_step2, 1 + n)
                    dve.tensor_scalar(q, wt2[0:w.shape[0], cols], -QMAX - 1, None, ALU.max)\
                        .then_inc(s.w_quantised, 1)

            def batch(b, par, half, first, last):
                nxt, nhalf = b + 1, half + par
                if not last and not first:
                    split_ctxT_hi(nxt, 1 - par, nhalf)
                split_ctx_lo(b, par)
                if first:
                    dve.wait_ge(s.bias_loaded, 48)
                    dve.tensor_tensor(xb[:, :, :], x_in[:, :, :],
                                      bout[:, :].unsqueeze(1).to_broadcast([TOK, PAIRS, D]), ALU.add)
                    dve.wait_ge(s.clip_exp, 1)
                    dve.tensor_scalar(sig127[:, :], sig127[:, :], 1.0, QMAX, ALU.add, ALU.mult)\
                        .then_inc(s.clip_step, 1)
                    dve.wait_ge(s.clip_step, 1)
                    dve.reciprocal(sig127[:, :], sig127[:, :]).then_inc(s.attn_made, 1)
                if last:
                    for step in range(5):
                        normalise(b - 1, 1 - par, step)
                    quantise_weights()
                    return
                for c in range(CHUNKS):
                    chunk(nxt, c)
                    if not first and 2 <= c <= 6:
                        normalise(b - 1, 1 - par, c - 2)
                    if not first and par == 0 and 8 <= c:
                        residual(half - 1, c - 8)
                    if c >= NM and c % NM == 0:
                        group(nxt, 1 - par, c // NM - 1)
                group(nxt, 1 - par, G - 1)
                split_ctxT_lo(nxt, 1 - par)
                if not first and par == 0:
                    layernorm2(half - 1)

            batches(dve, batch)
            dve.reduce_max(xmax[:, 0:3], xh[:, 0:3, :], AX.X, apply_absolute_value=True).then_inc(s.xmax3_step, 1)
            dve.wait_ge(s.xmax3_step, 1)
            dve.reduce_max(xmax[:, 2:3], xmax[:, 0:3], AX.X).then_inc(s.xmax_step, 1)
            normalise_last()
            for step in range(4):
                residual(PAIRS - 1, step, last=True)
            dve.wait_ge(s.ln2_step, 5 * PAIRS - 3)
            dve.tensor_scalar(x1_now[:, :], x1_now[:, :], mv2[:, 0:1], None, ALU.subtract).then_inc(s.xmax_step, 1)
            dve.wait_ge(s.xmax_step, 2)
            dve.reduce_max(xmax1[:, :], x1_now[:, :], AX.X, apply_absolute_value=True).then_inc(s.xmax_step, 1)
            dve.wait_ge(s.pow2_made, PAIRS)
            newton(dve, rstd2[:, :], nt2[:, :], veps2[:, :], s.ln2_step, 5 * (PAIRS - 1) + 2)
            dve.tensor_scalar(xmax[:, 3:4], xmax1[:, :], rstd2[:, :], -0.5, ALU.mult, ALU.mult).then_inc(s.xmax_step, 1)
            dve.tensor_scalar(xh[:, PAIRS - 1, :], x1_now[:, :], rstd2[:, :], -0.5, ALU.mult, ALU.mult)\
                .then_inc(s.xh_made, 1)
            dve.wait_ge(s.xmax_spread, 1)
            dve.reduce_max(xs[:, 0:1], p_mb[0][:, 0:2 * TOK], AX.X).then_inc(s.xmax_step, 1)
            dve.wait_ge(s.xmax_step, 5)
            dve.tensor_scalar(xs[:, 1:2], xs[:, 0:1], sig127[:, 0:1], None, ALU.mult).then_inc(s.xmax_step, 1)
            dve.wait_ge(s.xmax_step, 6)
            dve.reciprocal(xs[:, 2:3], xs[:, 1:2]).then_inc(s.xmax_step, 1)
            dve.tensor_scalar(xscale[:, :], wscale[:, 0:6], xs[:, 1:2], None, ALU.mult).then_inc(s.xscale_made, 1)
            own, others = HALVES
            dve.wait_ge(s.xmax_step, 7)
            dve.wait_ge(s.xhT_made, 1)
            dve.tensor_scalar(xt1[:, own], xh_banks[0][:, own], xs[:, 2:3], ROUND, ALU.mult, ALU.add)\
                .then_inc(s.xmax_step, 1)
            dve.wait_ge(s.xmax_step, 8)
            dve.tensor_scalar(xt2[:, own], xt1[:, own], ROUND, QMAX, ALU.subtract, ALU.min).then_inc(s.xmax_step, 1)
            dve.wait_ge(s.xmax_step, 9)
            dve.tensor_scalar(xq[:, own], xt2[:, own], -QMAX - 1, None, ALU.max)
            dve.wait_ge(s.x_raised, 2)
            dve.tensor_scalar(xq[:, others], xt2[:, others], QMAX + 1, QMAX, ALU.subtract, ALU.min)\
                .then_inc(s.x_quantised, 1)

            def multiply(f):
                fn = FT[f][1]
                dve.wait_ge(s.up_made, f + 1)
                dve.wait_ge(s.silu_made, f + 1)
                dve.scalar_tensor_tensor(hh[0:fn, f, :], u_banks[f][0:fn, 0:ALLTOK], xscale[0:fn, 3 + f:4 + f],
                                         silu[0:fn, f, :], ALU.mult, ALU.mult).then_inc(s.h_made, 1)

            def largest(k, f, cols=slice(0, ALLTOK)):
                fn = FT[f][1]
                return dve.reduce_max(hmax[0:fn, k:k + 1], hh[0:fn, f, cols], AX.X, apply_absolute_value=True)

            multiply(0)
            multiply(1)
            dve.wait_ge(s.h_made, 1)
            largest(0, 0)
            dve.wait_ge(s.h_made, 2)
            largest(1, 1)
            for k, cols in enumerate(HALVES):
                dve.wait_ge(s.last_h_made, k + 1)
                last = largest(2 + k, 2, cols)
            last.then_inc(s.h_step, 1)
            dve.wait_ge(s.h_step, 1)
            dve.reduce_max(hmax1[:, :], hmax[:, :], AX.X).then_inc(s.hmax_ready, 1)
            dve.wait_ge(s.hmax_spread, 1)
            dve.reduce_max(hs[:, 0:1], p_o[0][:, 0:128], AX.X).then_inc(s.h_step, 1)
            dve.wait_ge(s.h_step, 2)
            dve.tensor_scalar(hs[:, 1:2], hs[:, 0:1], sig127[:, 1:2], None, ALU.mult).then_inc(s.h_step, 1)
            dve.wait_ge(s.h_step, 3)
            dve.reciprocal(hs[:, 2:3], hs[:, 1:2]).then_inc(s.hs_made, 1)
            dve.wait_ge(s.hs_made, 1)
            for k, f in enumerate((0, 2)):
                fn = FT[f][1]
                dve.tensor_scalar(ht1[0:fn, f, :], hh[0:fn, f, :], hs[0:fn, 2:3], ROUND, ALU.mult, ALU.add)\
                    .then_inc(s.h_step, 1)
            dve.tensor_tensor(hs[:, 0:1], hs[:, 1:2], wscale[:, 6:7], ALU.mult).then_inc(s.y_step, 1)
            for k, f in enumerate((0, 2)):
                fn = FT[f][1]
                dve.wait_ge(s.h_step, 4 + k)
                dve.tensor_scalar(ht2[0:fn, f, :], ht1[0:fn, f, :], ROUND, QMAX, ALU.subtract, ALU.min)\
                    .then_inc(s.h_step2, 1)
            dve.wait_ge(s.h_step2, 1)
            dve.tensor_scalar(hq[:, 0, :], ht2[:, 0, :], -QMAX - 1, None, ALU.max).then_inc(s.h_quantised, 1)
            dve.wait_ge(s.h_raised, 2)
            dve.tensor_scalar(hq[:, 1, :], ht2[:, 1, :], QMAX + 1, QMAX, ALU.subtract, ALU.min)\
                .then_inc(s.h_quantised, 1)
            dve.wait_ge(s.h_step2, 2)
            dve.tensor_scalar(hq[0:96, 2, :], ht2[0:96, 2, :], -QMAX - 1, None, ALU.max).then_inc(s.h_quantised, 1)
            for k, cols in enumerate(HALVES):
                dve.wait_ge(s.y_made, k + 1)
                dve.scalar_tensor_tensor(y[:, cols], y_banks[k][:, 0:ALLTOK // 2], hs[:, 0:1], x1T[:, cols],
                                         ALU.mult, ALU.add).then_inc(s.y_step, 1)

        @block.tensor
        def _(pe):
            def busy(n, bank):
                for _ in range(n):
                    pe.matmul(bank[:, :], filler[:, :].to_broadcast([128, 128]),
                              filler[:, :].to_broadcast([128, 512]), start=True, stop=True)

            pe.wait_ge(s.filler_made, 1)
            busy(11, p_x)
            pe.wait_ge(s.qk_loaded, 32)
            for h in range(H):
                last = pe.matmul(p_mb[h // 4][:, (h % 4) * C:(h % 4 + 1) * C], wqT[:, h, :], wkT[:, h, :],
                                 start=True, stop=True)
                if h % 4 == 3:
                    last.then_inc(s.wqk_made, 1)
                if h == 3:
                    pe.wait_ge(s.ident_made, 2)
                    pe.wait_ge(s.xn_made, 1)
                    pe.transpose(p_mb[2][:, 0:TOK], xn[:, 0, :], ident[0:TOK, 0:TOK]).then_inc(s.xnT_made, 1)

            def max_chunk(b, par, c, first=False):
                g, k = c // NM, c % NM
                if c == 0:
                    pe.wait_ge(s.ctxT_hi_made, b + 1)
                if first or c == 0:
                    pe.wait_ge(s.q_copied, g + 1 if first else b + G)
                if not (first and c < NM):
                    pe.wait_ge(s.chunk_max_made, CHUNKS * b + c - NM + 1)
                pe.matmul(p_mb[k][0:GQ, 0:MC], q_now[par][0:C, g * GQ:(g + 1) * GQ],
                          ctxT_hi[par][0:C, k * MC:(k + 1) * MC], start=True, stop=True).then_inc(s.max_scored, 1)

            def scores(b, par, half, t, first):
                n = T * b + t
                if t == 0:
                    pe.wait_ge(s.ctxT_lo_made, b + 1)
                    if first:
                        pe.wait_ge(s.first_q_lo_made, 1)
                    else:
                        pe.wait_ge(max_moved[par], 16 * G * (half + 1))
                if not (first and t < 2):
                    pe.wait_ge(s.exp_made, 2 * (n - 1))
                keys = slice(t * KT, (t + 1) * KT)
                o = p_s[t % 2][0:KT, 0:HQ]
                pe.matmul(o, ctxT_lo[par][:, keys], q_now[par][0:C, :], start=True, stop=False)
                pe.matmul(o, ctxT_hi[par][0:C, keys], q_lo[:, bass.ds(b, 1), :].rearrange("c o n -> c (o n)"),
                          start=False, stop=False)
                if first and t == 0:
                    pe.wait_ge(max_moved[0], 16 * G)
                pe.matmul(o, ctxT_hi[par][:, keys], q_now[par][:, :], start=False, stop=True).then_inc(s.scored, 1)

            def weighted(b, par, t, early=False):
                n = T * b + t
                k = t % RING
                if t == 0:
                    pe.wait_ge(s.ctx_lo_made, b + 1)
                    if early:
                        pe.wait_ge(s.last_q_lo_made, DVE_HEADS)
                    else:
                        pe.wait_ge(s.attn_made, b)
                pe.wait_ge(s.exp_made, 2 * n + 1)
                pe.matmul(p_o[par][:, 0:HQ], ctx_hi[par][:, t, :], e_hi[:, k, :], start=(t == 0), stop=False,
                          skip_group_check=True)
                pe.matmul(p_o[par][0:C, 0:HQ], ctx_lo[par][:, t, :], e_hi[:, k, :], start=False, stop=False,
                          skip_group_check=True)
                pe.wait_ge(s.lo_made, n + 1)
                pe.matmul(p_o[par][:, 0:HQ], ctx_hi[par][:, t, :], e_lo[:, k, :], start=False, stop=(t == T - 1),
                          skip_group_check=True).then_inc(s.pv_done, 1)

            def project(p):
                pe.wait_ge(s.attn_made, 2 * p + 3)
                for h in range(H):
                    last = pe.matmul(p_x[0:TOK, 0:D], attn[:, h, :, :].rearrange("c b i -> c (b i)"), wvo[:, h, :],
                                     start=(h == 0), stop=(h == H - 1))
                last.then_inc(s.projected, 1)

            def project_last(p):
                for h in range(H):
                    pe.wait_ge(s.last_attn_made, 1 + h // 4)
                    last = pe.matmul(p_x[0:TOK, 0:D], attn[:, h, :, :].rearrange("c b i -> c (b i)"), wvo[:, h, :],
                                     start=(h == 0), stop=(h == H - 1))
                last.then_inc(s.projected, 1)

            def weights_vo(k):
                if k == 0:
                    pe.wait_ge(s.vo_loaded, 32)
                else:
                    pe.wait_ge(s.wvo_copied, k)
                for j in range(4):
                    last = pe.matmul(p_x[0:C, j * D:(j + 1) * D], wvT[:, 4 * k + j, :], wout[:, 4 * k + j, :],
                                     start=True, stop=True)
                last.then_inc(s.wvo_made, 1)

            def transpose_weights(k):
                o = p_mb[k].bitcast(BF16)
                for f, (f0, fn) in enumerate(FT):
                    if k < 2:
                        last = pe.transpose(o[:, f0:f0 + fn], (wg_q, wu_q)[k][0:fn, f, :], ident16[0:fn, 0:fn])
                    else:
                        last = pe.transpose(o[0:fn, f * D:(f + 1) * D], wd_q[:, f0:f0 + fn], ident16[:, :])
                last.then_inc(s.wT_made, 1)

            def query(h):
                if h < 4:
                    pe.wait_ge(s.first_q_full_made, h + 1)
                else:
                    pe.wait_ge(s.q_full_made, h - 3)
                pe.matmul(q_banks[h % 4][0:C, S:ALLTOK], wqk[:, h, :], xnT[:, S:ALLTOK], start=True, stop=True)\
                    .then_inc(s.q_made, 1)

            def row(g):
                return pe.matmul(p_x[C:C + 1, g * GQ:(g + 1) * GQ], maxima[0][:, g:g + 1], ident[0:GQ, 0:GQ],
                                 start=True, stop=True)

            busy(1, p_x)
            pe.wait_ge(s.xnT_copied, 1)
            for h in range(H):
                if h % 4 == 0:
                    pe.wait_ge(s.wqk_copied, h // 4 + 1)
                last = pe.matmul(q_banks[h // 2][0:C, (h % 2) * S:(h % 2 + 1) * S], wqk[:, h, :],
                                 xnT[:, 0:S], start=True, stop=True)
                if h % 2:
                    last.then_inc(s.first_q_made, 1)
            for p in range(1, PAIRS):
                pe.wait_ge(s.xn_made, p + 1)
                last = pe.transpose(p_x[:, p * TOK:(p + 1) * TOK], xn[:, p, :], ident[0:TOK, 0:TOK])
            last.then_inc(s.xnT_made, 1)
            heads = iter(range(H))
            for g, n_heads in enumerate(FIRST_QUERY_PLAN):
                for k in range(NM):
                    max_chunk(0, 0, NM * g + k, first=True)
                if g == 0:
                    pe.wait_ge(s.xnT_copied, 2)
                for k in range(n_heads):
                    if g == G - 1 and k == 1:
                        pe.wait_ge(s.max_made, G - 1)
                        for i in range(G - 1):
                            last = row(i)
                        last.then_inc(s.row_made, 1)
                    query(next(heads))
            pe.wait_ge(s.ones_made, 2)
            pe.wait_ge(max_moved[0], 8 * G)
            pe.wait_ge(s.max_made, G)
            row(G - 1).then_inc(s.row_made, 1)

            def batch(b, par, half, first, last):
                for t in range(T):
                    scores(b, par, half, t, first)
                    plan = FIRST_CHUNK_PLAN if first else CHUNK_PLAN
                    if not last:
                        for c in range(sum(plan[:t]), sum(plan[:t + 1])):
                            max_chunk(b + 1, 1 - par, c)
                    if not first and par == 0 and t == 6:
                        project(half - 1)
                    if first and t in (1, 5):
                        weights_vo(t // 4)
                    if t >= LAG:
                        weighted(b, par, t - LAG, early=first)
                    elif not first:
                        weighted(b - 1, 1 - par, T - LAG + t)

            batch(0, 0, 0, True, False)
            pe.wait_ge(s.q_lo_made, H - DVE_HEADS)
            pe.wait_ge(s.ones_made, 4)
            with pe.Fori(1, PAIRS) as i:
                batch(2 * i - 1, 1, i - 1, False, False)
                batch(2 * i, 0, i, False, False)
            batch(B - 1, 1, PAIRS - 1, False, True)
            pe.wait_ge(s.w_quantised, 7)
            for t in range(T - LAG, T):
                transpose_weights(t - (T - LAG))
                weighted(B - 1, 1, t)
            pe.wait_ge(s.xh_made, PAIRS - 1)
            pe.wait_ge(s.x1_kept, PAIRS - 1)
            for p in range(PAIRS - 1):
                pe.transpose(xh_banks[p // 2][:, p * TOK:(p + 1) * TOK], xh[:, p, :], ident[0:TOK, 0:TOK])
                pe.transpose(p_s[0][:, p * TOK:(p + 1) * TOK], x1[:, p, :], ident[0:TOK, 0:TOK])
            pe.wait_ge(s.wT_copied, 3)
            pe.wait_ge(s.xmax_step, 1)
            pe.matmul(p_mb[0][:, 0:TOK], xmax[:, 2:3].to_broadcast([TOK, 128]), ident[0:TOK, 0:TOK],
                      start=True, stop=True)
            busy(4, p_mb[1])
            project_last(PAIRS - 1)
            busy(10, p_mb[1])
            pe.wait_ge(s.xmax_step, 4)
            pe.matmul(p_mb[0][:, TOK:2 * TOK], xmax[:, 3:4].to_broadcast([TOK, 128]), ident[0:TOK, 0:TOK],
                      start=True, stop=True).then_inc(s.xmax_spread, 1)
            pe.wait_ge(s.xh_made, PAIRS)
            pe.transpose(xh_banks[1][:, (PAIRS - 1) * TOK:PAIRS * TOK], xh[:, PAIRS - 1, :], ident[0:TOK, 0:TOK])\
                .then_inc(s.xhT_made, 1)
            pe.wait_ge(s.x1_kept, PAIRS)
            pe.transpose(p_s[0][:, (PAIRS - 1) * TOK:PAIRS * TOK], x1[:, PAIRS - 1, :], ident[0:TOK, 0:TOK])\
                .then_inc(s.x1T_made, 1)
            busy(6, p_mb[1])
            pe.wait_ge(s.x1T_copied, 1)
            pe.wait_ge(s.x_quantised, 1)
            for f, (f0, fn) in enumerate(FT):
                pe.matmul(g_banks[f][0:fn, 0:ALLTOK], wgT[:, f0:f0 + fn], xq[:, :], start=True, stop=True)\
                    .then_inc(s.gate_made, 1)
                pe.matmul(u_banks[f][0:fn, 0:ALLTOK], wuT[:, f0:f0 + fn], xq[:, :], start=True, stop=True)\
                    .then_inc(s.up_made, 1)
            busy(12, p_o[1])
            pe.wait_ge(s.hmax_ready, 1)
            pe.matmul(p_o[0][:, 0:128], hmax1[:, 0:1].to_broadcast([128, 128]), ident[:, :],
                      start=True, stop=True).then_inc(s.hmax_spread, 1)
            busy(8, p_o[1])
            for f, (f0, fn) in enumerate(FT):
                pe.wait_ge(s.h_quantised, f + 1)
                for k, cols in enumerate(HALVES):
                    last = pe.matmul(y_banks[k][:, 0:ALLTOK // 2], wdT[0:fn, f, :], hq[0:fn, f, cols],
                                     start=(f == 0), stop=(f == 2))
                    if f == 2:
                        last.then_inc(s.y_made, 1)


def newton(dve, r, t, v, step, n):
    dve.tensor_tensor(t, r, r, ALU.mult).then_inc(step, 1)
    dve.wait_ge(step, n + 1)
    dve.tensor_tensor(t, t, v, ALU.mult).then_inc(step, 1)
    dve.wait_ge(step, n + 2)
    dve.scalar_tensor_tensor(r, t, 3.0, r, ALU.subtract, ALU.mult).then_inc(step, 1)
    dve.wait_ge(step, n + 3)


def kernel(x, ctx_768, L0_xattn_Wq, L0_xattn_Wk, L0_xattn_Wv, L0_xattn_Wout, L0_xattn_bout,
           L0_ffn_clip_x, L0_ffn_clip_down, L0_ffn_w_gate, L0_ffn_w_up, L0_ffn_w_down):
    import numpy as np
    from concourse import bacc
    from concourse.bass_utils import run_bass_kernel_spmd

    a = {k: np.asarray(v) for k, v in locals().items() if k not in ("np", "bacc", "run_bass_kernel_spmd")}
    ctx = a["ctx_768"]
    arrays = {
        "x_in_d": a["x"].reshape(PAIRS, TOK, D).transpose(1, 0, 2),
        "ctxT_d": ctx.transpose(0, 2, 1),
        "ctx_d": ctx.reshape(B, T, KT, C).transpose(0, 2, 1, 3).reshape(B, KT, T * C),
        "wqT_d": a["L0_xattn_Wq"].reshape(D, H, DH).transpose(2, 1, 0),
        "wkT_d": a["L0_xattn_Wk"].reshape(C, H, DH).transpose(2, 1, 0),
        "wvT_d": a["L0_xattn_Wv"].reshape(C, H, DH).transpose(2, 1, 0),
        "wout_d": a["L0_xattn_Wout"].reshape(H, DH, D).transpose(1, 0, 2),
        "bout_d": np.broadcast_to(a["L0_xattn_bout"][None], (TOK, D)),
        "clipx_d": np.broadcast_to(a["L0_ffn_clip_x"][None], (128, 1)),
        "clipd_d": np.broadcast_to(a["L0_ffn_clip_down"][None], (128, 1)),
        "wg_d": a["L0_ffn_w_gate"], "wu_d": a["L0_ffn_w_up"], "wd_d": a["L0_ffn_w_down"],
    }
    arrays = {k: np.ascontiguousarray(v) for k, v in arrays.items()}
    nc = bacc.Bacc("TRN2", target_bir_lowering=False, num_devices=1)
    args = [nc.dram_tensor(k, v.shape, mybir.dt.from_np(v.dtype), kind="ExternalInput").ap() for k, v in arrays.items()]
    out = nc.dram_tensor("out_d", (D, ALLTOK), F32, kind="ExternalOutput").ap()
    program(nc, *args, out)
    r = run_bass_kernel_spmd(nc, [arrays], core_ids=[0])
    got = r.results[0]["out_d"]
    return got.T.reshape(B, S, D)
```
